# Optimizing a Trainium2 kernel written in Bass

```python
import numpy as np
import jax
import jax.numpy as jnp

def _softmax(x, axis=-1):
    return jax.nn.softmax(x, axis=axis)

def _gelu(x):
    return jax.nn.gelu(x, approximate=True)

def _silu(x):
    return jax.nn.silu(x)

def _sigmoid(x):
    return jax.nn.sigmoid(x)

def _layernorm(x, axis=-1, eps=1e-05):
    m = jnp.mean(x, axis=axis, keepdims=True)
    v = jnp.var(x, axis=axis, keepdims=True)
    return (x - m) / jnp.sqrt(v + eps)

def _scatter_add(tgt, idx, src, axis=0):
    return tgt.at[idx].add(src)

def _segment_sum(src, seg, n):
    return jax.ops.segment_sum(src, seg, n)
kernel_name = 'mk_seq_postln_d1_jaxref_r4_009a3d'

def setup_inputs(seed: int=0):
    np.random.seed(seed)
    _w = jnp.asarray

    def _L0_attn_setup():
        import jax, jax.numpy as jnp
        import numpy as np
        DIM = 256
        D_STATE = 16
        D_CONV = 4
        EXPAND = 2
        D_INNER = EXPAND * DIM
        BATCH = 4
        SEQ = 512

        def _reference_tuple_inner(x, in_proj_w, conv_w, x_proj_w, dt_proj_w, dt_proj_b, A_log, D, out_proj_w, norm_w, norm_b):
            Bsz, L, _ = x.shape
            shortcut = x
            mu = jnp.mean(x, axis=-1, keepdims=True)
            var = jnp.var(x, axis=-1, keepdims=True)
            h = (x - mu) / jnp.sqrt(var + 1e-05) * norm_w + norm_b
            h = h @ in_proj_w.T
            hp = jnp.pad(h, ((0, 0), (D_CONV - 1, 0), (0, 0)))
            h_conv = sum((hp[:, k:k + L, :] * conv_w[:, k] for k in range(D_CONV)))
            h = jax.nn.silu(h_conv)
            proj = h @ x_proj_w.T
            dt_in = proj[..., :1]
            B_param = proj[..., 1:1 + D_STATE]
            C_param = proj[..., 1 + D_STATE:]
            dt = jax.nn.softplus(dt_in @ dt_proj_w.T + dt_proj_b)
            A = -jnp.exp(A_log)

            def step(state, inp):
                dt_t, B_t, C_t, x_t = inp
                state = jnp.exp(A[None] * dt_t[:, :, None]) * state + B_t[:, None, :] * x_t[:, :, None]
                y = jnp.einsum('bnd,bd->bn', state, C_t) + D * x_t
                return (state, y)
            init = jnp.zeros((Bsz, D_INNER, D_STATE), x.dtype)
            xs = (jnp.swapaxes(dt, 0, 1), jnp.swapaxes(B_param, 0, 1), jnp.swapaxes(C_param, 0, 1), jnp.swapaxes(h, 0, 1))
            state, ys = jax.lax.scan(step, init, xs)
            y = jnp.swapaxes(ys, 0, 1)
            out = jax.nn.silu(y) @ out_proj_w.T + shortcut
            return (out, state)
        key = jax.random.key(seed)
        ks = jax.random.split(key, 9)
        n = lambda i, shape, scale=0.02: jax.random.normal(ks[i], shape, jnp.float32) * scale
        return {'x': jax.random.normal(ks[0], (BATCH, SEQ, DIM), jnp.float32), 'in_proj_w': n(1, (D_INNER, DIM)), 'conv_w': n(2, (D_INNER, D_CONV), 0.1), 'x_proj_w': n(3, (2 * D_STATE + 1, D_INNER)), 'dt_proj_w': n(4, (D_INNER, 1), 1.0), 'dt_proj_b': n(5, (D_INNER,), 0.1), 'A_log': jax.random.normal(ks[6], (D_INNER, D_STATE), jnp.float32), 'D': jnp.ones((D_INNER,), jnp.float32), 'out_proj_w': n(7, (DIM, D_INNER)), 'norm_w': jnp.ones((DIM,), jnp.float32), 'norm_b': jnp.zeros((DIM,), jnp.float32)}
    _L0_attn_in = _L0_attn_setup()

    def _L0_ffn_setup():
        import jax, jax.numpy as jnp
        import numpy as np
        B, S, D, H, E, K = (4, 512, 256, 1024, 8, 2)
        CAPACITY_FACTOR = 1.5
        C = int(CAPACITY_FACTOR * B * S * K / E)
        key = jax.random.key(seed)
        ks = jax.random.split(key, 6)
        x = jax.random.normal(ks[0], (B, S, D), dtype=jnp.float32)
        w_router = jax.random.normal(ks[1], (D, E), dtype=jnp.float32) * 0.02
        w1 = jax.random.normal(ks[2], (E, D, H), dtype=jnp.float32) * 0.02
        b1 = jnp.zeros((E, H), dtype=jnp.float32)
        w2 = jax.random.normal(ks[3], (E, H, D), dtype=jnp.float32) * 0.02
        b2 = jnp.zeros((E, D), dtype=jnp.float32)
        return {'x': x, 'w_router': w_router, 'w1': w1, 'b1': b1, 'w2': w2, 'b2': b2}
    _L0_ffn_in = _L0_ffn_setup()
    _d = {'L0_attn_x': _L0_attn_in['x'], 'L0_attn_in_proj_w': _L0_attn_in['in_proj_w'], 'L0_attn_conv_w': _L0_attn_in['conv_w'], 'L0_attn_x_proj_w': _L0_attn_in['x_proj_w'], 'L0_attn_dt_proj_w': _L0_attn_in['dt_proj_w'], 'L0_attn_dt_proj_b': _L0_attn_in['dt_proj_b'], 'L0_attn_A_log': _L0_attn_in['A_log'], 'L0_attn_D': _L0_attn_in['D'], 'L0_attn_out_proj_w': _L0_attn_in['out_proj_w'], 'L0_attn_norm_w': _L0_attn_in['norm_w'], 'L0_attn_norm_b': _L0_attn_in['norm_b'], 'L0_ffn_w_router': _L0_ffn_in['w_router'], 'L0_ffn_w1': _L0_ffn_in['w1'], 'L0_ffn_b1': _L0_ffn_in['b1'], 'L0_ffn_w2': _L0_ffn_in['w2'], 'L0_ffn_b2': _L0_ffn_in['b2']}
    _x0 = _d['L0_attn_x']
    _d['L0_attn_x'] = jax.random.normal(jax.random.fold_in(jax.random.key(seed), 1), (1, 4096, 256), dtype=_x0.dtype)
    del _x0
    return _d

def reference(L0_attn_x, L0_attn_in_proj_w, L0_attn_conv_w, L0_attn_x_proj_w, L0_attn_dt_proj_w, L0_attn_dt_proj_b, L0_attn_A_log, L0_attn_D, L0_attn_out_proj_w, L0_attn_norm_w, L0_attn_norm_b, L0_ffn_w_router, L0_ffn_w1, L0_ffn_b1, L0_ffn_w2, L0_ffn_b2):

    def _L0_attn_ref(x, in_proj_w, conv_w, x_proj_w, dt_proj_w, dt_proj_b, A_log, D, out_proj_w, norm_w, norm_b):
        import jax, jax.numpy as jnp
        import numpy as np
        DIM = 256
        D_STATE = 16
        D_CONV = 4
        EXPAND = 2
        D_INNER = EXPAND * DIM
        BATCH = 4
        SEQ = 512

        def _reference_tuple_inner(x, in_proj_w, conv_w, x_proj_w, dt_proj_w, dt_proj_b, A_log, D, out_proj_w, norm_w, norm_b):
            Bsz, L, _ = x.shape
            shortcut = x
            mu = jnp.mean(x, axis=-1, keepdims=True)
            var = jnp.var(x, axis=-1, keepdims=True)
            h = (x - mu) / jnp.sqrt(var + 1e-05) * norm_w + norm_b
            h = h @ in_proj_w.T
            hp = jnp.pad(h, ((0, 0), (D_CONV - 1, 0), (0, 0)))
            h_conv = sum((hp[:, k:k + L, :] * conv_w[:, k] for k in range(D_CONV)))
            h = jax.nn.silu(h_conv)
            proj = h @ x_proj_w.T
            dt_in = proj[..., :1]
            B_param = proj[..., 1:1 + D_STATE]
            C_param = proj[..., 1 + D_STATE:]
            dt = jax.nn.softplus(dt_in @ dt_proj_w.T + dt_proj_b)
            A = -jnp.exp(A_log)

            def step(state, inp):
                dt_t, B_t, C_t, x_t = inp
                state = jnp.exp(A[None] * dt_t[:, :, None]) * state + B_t[:, None, :] * x_t[:, :, None]
                y = jnp.einsum('bnd,bd->bn', state, C_t) + D * x_t
                return (state, y)
            init = jnp.zeros((Bsz, D_INNER, D_STATE), x.dtype)
            xs = (jnp.swapaxes(dt, 0, 1), jnp.swapaxes(B_param, 0, 1), jnp.swapaxes(C_param, 0, 1), jnp.swapaxes(h, 0, 1))
            state, ys = jax.lax.scan(step, init, xs)
            y = jnp.swapaxes(ys, 0, 1)
            out = jax.nn.silu(y) @ out_proj_w.T + shortcut
            return (out, state)
        return _reference_tuple_inner(x, in_proj_w, conv_w, x_proj_w, dt_proj_w, dt_proj_b, A_log, D, out_proj_w, norm_w, norm_b)[0]

    def _L0_ffn_ref(x, w_router, w1, b1, w2, b2):
        import jax, jax.numpy as jnp
        import numpy as np
        B, S, D, H, E, K = (4, 512, 256, 1024, 8, 2)
        CAPACITY_FACTOR = 1.5
        C = int(CAPACITY_FACTOR * B * S * K / E)
        Bs, Ss, Ds = x.shape
        N = Bs * Ss
        xf = x.reshape(N, Ds)
        logits = xf @ w_router
        probs = jax.nn.softmax(logits, axis=-1)
        gate, eidx = jax.lax.top_k(probs, K)
        gate = gate / jnp.sum(gate, axis=-1, keepdims=True)
        oh = jax.nn.one_hot(eidx, E, dtype=jnp.float32)
        ohf = oh.reshape(N * K, E)
        pos = jnp.cumsum(ohf, axis=0) - 1.0
        posk = jnp.sum(pos * ohf, axis=-1).reshape(N, K).astype(jnp.int32)
        keep = posk < C
        gate = gate * keep.astype(gate.dtype)
        e_flat = eidx.reshape(-1)
        p_flat = jnp.where(keep, posk, 0).reshape(-1)
        contrib = (xf[:, None, :] * keep[..., None].astype(xf.dtype)).reshape(N * K, Ds)
        expert_in = jnp.zeros((E, C, Ds), dtype=xf.dtype).at[e_flat, p_flat].add(contrib)
        h = jax.nn.relu(jnp.einsum('ecd,edh->ech', expert_in, w1) + b1[:, None, :])
        expert_out = jnp.einsum('ech,eho->eco', h, w2) + b2[:, None, :]
        tok = expert_out[e_flat, p_flat].reshape(N, K, -1)
        y = jnp.sum(tok * gate[..., None], axis=1)
        return y.reshape(Bs, Ss, -1)
    x = L0_attn_x
    x = _layernorm(x + _L0_attn_ref(x, L0_attn_in_proj_w, L0_attn_conv_w, L0_attn_x_proj_w, L0_attn_dt_proj_w, L0_attn_dt_proj_b, L0_attn_A_log, L0_attn_D, L0_attn_out_proj_w, L0_attn_norm_w, L0_attn_norm_b), axis=-1)
    x = _layernorm(x + _L0_ffn_ref(x, L0_ffn_w_router, L0_ffn_w1, L0_ffn_b1, L0_ffn_w2, L0_ffn_b2), axis=-1)
    return x

_drawn_inputs = setup_inputs


def setup_inputs(seed=0):
    import zlib

    import numpy as np

    out = dict(_drawn_inputs(seed))
    spreads = {'L0_attn_D': (1.0, 0.6),
     'L0_attn_norm_w': (1.0, 0.6),
     'L0_attn_norm_b': (0.0, 0.8),
     'L0_ffn_b1': (0.0, 0.289),
     'L0_ffn_b2': (0.0, 0.1)}
    factors = {'L0_attn_in_proj_w': 6.204,
     'L0_attn_conv_w': 8.0,
     'L0_attn_x_proj_w': 8.0,
     'L0_attn_dt_proj_w': 8.0,
     'L0_attn_dt_proj_b': 8.0,
     'L0_attn_A_log': 8.0,
     'L0_attn_out_proj_w': 6.863}
    for name, (base, spread) in spreads.items():
        noise = np.random.default_rng([zlib.crc32(name.encode()), seed]).standard_normal(out[name].shape)
        drawn = base * np.exp(spread * noise) if base else spread * noise
        out[name] = jnp.asarray(drawn.astype(out[name].dtype))
    for name, factor in factors.items():
        out[name] = (out[name] * factor).astype(out[name].dtype)
    return out
```

```python
from contextlib import ExitStack

import concourse.bass as bass
from concourse import mybir

F32 = mybir.dt.float32
F32R = mybir.dt.float32r
U32 = mybir.dt.uint32
U8 = mybir.dt.uint8
ALU = mybir.AluOpType
ACT = mybir.ActivationFunctionType
AX = mybir.AxisListType

P = 128
L = 4096
D = 256
DI = 512
NS = 16
KC = 4
T = 512
NC = L // T
TJ = T // P
DB = DI // P
KD = D // P
UNITS = NS * DB
E = 8
H = 1024
HB = H // P
TOPK = 2
CAP = int(1.5 * 4 * 512 * TOPK / E)
CT = CAP // P
SLOTS = E * CAP
EPS = 1e-5
ROUTE = 35
ZEROS = SLOTS * D // (P * 1024)
N_PARAMS = 13
TINY = 2.0 ** -8

C_ID, C_TRI, C_ONE, C_RANK, C_BASE, C_TRASH, C_END = 0, 128, 256, 384, 416, 480, 544

A_USES = ["xT0", "xT1", "in0", "in1", "in2", "in3", "xp", "dtb"]
Q_USES = ["op0", "op1", "x1T0", "x1T1", "rt", "pos"]
ALL_USES = ["xT0", "xT1", "in0", "in1", "in2", "in3", "op0", "op1", "x1T0", "xp", "x1T1", "dtb", "rt", "pos"]


class Step:

    def __init__(self, c, par, a=True, scan=True, q=True):
        self.c, self.par, self.a, self.scan, self.q = c, par, a, scan, q
        self.uses = [u for u in ALL_USES if (a and u in A_USES) or (q and u in Q_USES)]
        if not q:
            self.base = len(A_USES) * (c + 1)
        else:
            self.base = 2 * len(A_USES) + len(ALL_USES) * (c - 1)
            if not a and not scan:
                self.base = 2 * len(A_USES) + len(ALL_USES) * (NC - 2) + len(Q_USES)

    def before(self, use):
        return self.base + self.uses.index(use)


def steps_of(engine_loop, body):
    body(Step(-1, 1, scan=False, q=False))
    body(Step(0, 0, q=False))
    with engine_loop(1, NC - 2, 2) as c:
        body(Step(c, 1))
        body(Step(c + 1, 0))
    body(Step(NC - 1, (NC - 1) % 2, a=False))
    body(Step(NC, NC % 2, a=False, scan=False))


def wait(eng, sem, value):
    if not isinstance(value, int) or value > 0:
        eng.wait_ge(sem, value)


def hold(eng, passed):
    eng.sem_inc(passed, 1)


def mixer_and_routing(nc, io, scr, gates, slot_of):
    with ExitStack() as ctx:
        def sb(name, shape, dt=F32):
            return ctx.enter_context(nc.sbuf_tensor(name, shape, dt))

        def ps(name, shape):
            return ctx.enter_context(nc.psum_tensor(name, shape, F32))

        def sem(name):
            return ctx.enter_context(nc.semaphore(name))

        cst = sb("cst", [P, C_END])
        ident, tri, ones = cst[:, C_ID:C_ID + P], cst[:, C_TRI:C_TRI + P], cst[:, C_ONE:C_ONE + P]
        rank = cst[:, C_RANK:C_RANK + 32].rearrange("p (j e) -> p j e", e=E)
        base8 = cst[:, C_BASE:C_BASE + 64].rearrange("p (k e) -> p k e", e=E)
        w_in = sb("w_in", [P, KD, DI])
        w_out = sb("w_out", [P, DB, D])
        w_x = sb("w_x", [P, DB, 2 * NS + 1])
        w_r = sb("w_r", [P, KD, E])
        sel_raw = sb("sel_raw", [2 * NS + 1, (NS + 1) * P])
        sel = sb("sel", [2 * NS + 1, (NS + 1) * P], F32R)
        a_neg = sb("a_neg", [P, DB, NS])
        conv_w = sb("conv_w", [P, DB, KC])
        dt_w = sb("dt_w", [P, DB])
        dt_b = sb("dt_b", [P, DB])
        d_skip = sb("d_skip", [P, DB])
        n_w = sb("n_w", [P, KD])
        n_b = sb("n_b", [P, KD])
        neg_half = sb("neg_half", [P, TJ])
        zeros = sb("zeros", [P, 1024])
        xt = sb("xt", [P, TJ, D])
        st_a = sb("st_a", [P, TJ, 6])
        mv_a = sb("mv_a", [P, TJ, 2])
        ve_a = sb("ve_a", [P, TJ])
        rs_a = sb("rs_a", [P, TJ])
        xn = sb("xn", [P, TJ, D])
        xnT = sb("xnT", [P, KD, T])
        hin = sb("hin", [P, DB, T + KC - 1])
        cv = sb("cv", [P, DB, T])
        h = [sb(f"h{i}", [P, DB, T]) for i in range(2)]
        dt = [sb(f"dt{i}", [P, DB, T]) for i in range(2)]
        bcf = sb("bcf", [2 * NS + 1, T])
        bc_hi = [sb(f"bc_hi{i}", [2 * NS + 1, T], F32R) for i in range(2)]
        bc_lo = [sb(f"bc_lo{i}", [2 * NS + 1, T], F32R) for i in range(2)]
        z = sb("z", [P, DB, T])
        ez = sb("ez", [P, DB, T])
        ser = sb("ser", [P, DB, T])
        small = sb("small", [P, DB, T], U8)
        da = sb("da", [P, 4, T])
        state = sb("state", [P, 2, DB, T])
        carry = sb("carry", [P, NS, DB])
        prod = sb("prod", [P, 4, T])
        c_row = sb("c_row", [P, 2, 4, T])
        yv = sb("yv", [P, DB, T])
        xr = sb("xr", [P, TJ, D])
        st_q = sb("st_q", [P, TJ, 6])
        mv_q = sb("mv_q", [P, TJ, 2])
        ve_q = sb("ve_q", [P, TJ])
        rs_q = sb("rs_q", [P, TJ])
        x1 = sb("x1", [P, TJ, D])
        x1T = sb("x1T", [P, KD, T])
        mx = sb("mx", [P, TJ])
        lg = sb("lg", [P, TJ, E])
        ex = sb("ex", [P, TJ, E])
        su = sb("su", [P, TJ])
        rsu = sb("rsu", [P, TJ])
        pr = sb("pr", [P, TJ, E])
        pr2 = sb("pr2", [P, TJ, E])
        pk = sb("pk", [P, TOPK, TJ])
        eq = sb("eq", [P, TJ, E])
        wr = sb("wr", [P, TJ, E])
        wm = sb("wm", [P, TJ])
        oh = sb("oh", [P, TOPK, TJ, E])
        hot = sb("hot", [P, TJ, E])
        hot_sum = sb("hot_sum", [P, E])
        hot_before = sb("hot_before", [P, E])
        po = sb("po", [P, TOPK * TJ, E])
        bo = sb("bo", [P, TOPK * TJ, E])
        pos_k = sb("pos_k", [P, TOPK * TJ])
        base_k = sb("base_k", [P, TOPK * TJ])
        keep = sb("keep", [P, TOPK * TJ])
        den = sb("den", [P, TJ])
        rden = sb("rden", [P, TJ])
        gk = sb("gk", [P, TOPK, TJ])
        kpos = sb("kpos", [P, TOPK * TJ])
        far = sb("far", [P, TOPK * TJ])
        sidx = sb("sidx", [P, TOPK * TJ], U32)

        y_ps = ps("y_ps", [P, DB, T])
        b_ps = ps("b_ps", [P, T])
        u_ps = ps("u_ps", [P, 2, T])
        m_ps = ps("m_ps", [P, T])

        passed = [sem(f"passed_{n}") for n in ("sp", "pool", "dve")]
        params = sem("params")
        setup = sem("setup")
        neg_set = sem("neg_set")
        pool_set = sem("pool_set")
        x_in = sem("x_in")
        xr_in = sem("xr_in")
        c_out = sem("c_out")
        c_in = [sem("c_in0"), sem("c_in1")]
        x1_out = sem("x1_out")
        slotted = sem("slotted")
        filled = sem("filled")
        stat_a = sem("stat_a")
        rstd_a = sem("rstd_a")
        xnT_set = sem("xnT_set")
        hin_set = sem("hin_set")
        conv = sem("conv")
        halo = sem("halo")
        h_set = sem("h_set")
        bc_set = sem("bc_set")
        z_set = sem("z_set")
        soft = sem("soft")
        series = sem("series")
        dt_set = sem("dt_set")
        da_set = sem("da_set")
        b_set = sem("b_set")
        u_set = sem("u_set")
        scan = sem("scan")
        carried = sem("carried")
        prod_set = sem("prod_set")
        summed = sem("summed")
        y_out = sem("y_out")
        y_silu = sem("y_silu")
        res = sem("res")
        rstd_q = sem("rstd_q")
        x1T_set = sem("x1T_set")
        route = sem("route")
        e_set = sem("e_set")

        block = ctx.enter_context(nc.Block())
        x_dram, expert_in, x1_dram, c_dram = io["x"], scr["expert_in"], scr["x1"], scr["c"]

        def tokens(c):
            return bass.ds(c * T, T)

        @block.sync
        def _(sp):
            for dst, src in ((cst[:, :], io["consts"]), (w_in[:, :, :], io["w_in"].rearrange("(k p) n -> p k n", p=P)),
                             (w_out[:, :, :], io["w_out"].rearrange("(k p) n -> p k n", p=P)),
                             (w_x[:, :, :], io["w_x"].rearrange("(k p) n -> p k n", p=P)),
                             (w_r[:, :, :], io["w_router"].rearrange("(k p) n -> p k n", p=P)),
                             (sel_raw[:, :], io["sel"]),
                             (a_neg[:, :, :], io["a_log"].rearrange("(k p) n -> p k n", p=P)),
                             (conv_w[:, :, :], io["conv_w"].rearrange("(k p) n -> p k n", p=P)),
                             (dt_w[:, :], io["dt_w"]), (dt_b[:, :], io["dt_b"]), (d_skip[:, :], io["d_skip"]),
                             (n_w[:, :], io["n_w"]), (n_b[:, :], io["n_b"])):
                sp.dma_start(dst, src).then_inc(params, 16)
            sp.sem_inc(x1_out, 1)

            def c_rows(c, q):
                wait(sp, prod_set, c * UNITS + 16 * (q - 1))
                sp.dma_start(c_row[:, q % 2, :, :], c_dram[4 * q:4 * q + 4, tokens(c)].partition_broadcast(P)
                             ).then_inc(c_in[q % 2], 16)

            def body(s):
                c = s.c
                if s.a:
                    wait(sp, stat_a, 3 * (c + 1))
                    sp.dma_start(xt[:, :, :], x_dram[tokens(c + 1), :].rearrange("(j p) d -> p j d", p=P)
                                 ).then_inc(x_in, 16)
                if s.q:
                    sp.wait_ge(res, 1 + 5 * (c - 1))
                    sp.dma_start(xr[:, :, :], x_dram[tokens(c - 1), :].rearrange("(j p) d -> p j d", p=P)
                                 ).then_inc(xr_in, 16)
                if s.scan:
                    c_rows(c, 1)
                    c_rows(c, 2)
                if s.q:
                    sp.wait_ge(res, 1 + 5 * c)
                    sp.dma_start(x1_dram[tokens(c - 1), :].rearrange("(j p) d -> p j d", p=P), x1[:, :, :]
                                 ).then_inc(x1_out, 16)
                if s.scan:
                    c_rows(c, 3)
                if s.a:
                    sp.wait_ge(bc_set, 3 * (c + 1) + 1)
                    hold(sp, passed[0])
                    sp.dma_start(c_dram[:, tokens(c + 1)], bcf[NS + 1:2 * NS + 1, :]).then_inc(c_out, 16)
                    sp.wait_ge(c_out, 16 * (c + 2))
                    c_rows(c + 1, 0)

            steps_of(sp.Fori, body)
            sp.wait_ge(x1_out, 1 + 16 * NC)

        @block.gpsimd
        def _(pool):
            pool.memset(neg_half[:, :], -0.5).then_inc(pool_set, 1)
            pool.memset(zeros[:, :], 0.0).then_inc(pool_set, 1)
            pool.memset(carry[:, :, :], 0.0).then_inc(pool_set, 1)
            pool.memset(hot_before[:, :], 0.0).then_inc(pool_set, 1)
            pool.memset(hot_sum[:, :], 0.0).then_inc(pool_set, 1)
            pool.memset(hin[:, :, 0:KC - 1], 0.0).then_inc(pool_set, 1)

            pool.wait_ge(pool_set, 2)
            slots = expert_in[0:SLOTS, :].rearrange("(p r) d -> p (r d)", p=P)
            for k in range(ZEROS):
                pool.dma_start(slots[:, k * 1024:(k + 1) * 1024], zeros[:, :]).then_inc(slotted, 16)

            def unit(s, u):
                n, db = divmod(u, DB)
                g = s.c * UNITS + u
                if u % 16 == 0:
                    q = n // 4
                    pool.wait_ge(c_in[q % 2], 16 * (2 * s.c + q // 2 + 1))
                pool.wait_ge(scan, g + 1)
                wait(pool, summed, g - 3)
                pool.tensor_tensor(prod[:, u % 4, :], state[:, n % 2, db, :], c_row[:, (n // 4) % 2, n % 4, :],
                                   ALU.mult).then_inc(prod_set, 1)

            def rstd(src, ve, rs, done, ready, need, k):
                pool.wait_ge(ready, need)
                hold(pool, passed[1])
                pool.tensor_scalar(ve[:, :], src[:, :, 1], EPS, None, ALU.add).then_inc(done, 1)
                pool.wait_ge(done, 2 * k + 1)
                pool.tensor_tensor(rs[:, :], ve[:, :], neg_half[:, :], ALU.pow).then_inc(done, 1)

            def softplus_series(s):
                c = s.c
                pool.wait_ge(soft, 3 * (c + 1) + 2)
                wait(pool, dt_set, 3 * (c + 1))
                hold(pool, passed[1])
                pool.tensor_scalar(ser[:, :, :], ez[:, :, :], -0.5, 1.0, ALU.mult, ALU.add).then_inc(series, 1)
                pool.wait_ge(series, 2 * (c + 1) + 1)
                pool.tensor_tensor(ser[:, :, :], ser[:, :, :], ez[:, :, :], ALU.mult).then_inc(series, 1)

            def scatter(s):
                c = s.c
                pool.wait_ge(route, ROUTE * c)
                pool.wait_ge(slotted, 16 * ZEROS)
                hold(pool, passed[1])
                for k in range(TOPK):
                    for j in range(TJ):
                        col = k * TJ + j
                        pool.indirect_dma_start(expert_in[:, :], bass.IndirectOffsetOnAxis(sidx[:, col:col + 1], 0),
                                                x1[:, j, :], None).then_inc(slotted, 16)

            def body(s):
                for u in range(UNITS if s.scan else 1):
                    if s.scan:
                        unit(s, u)
                    if s.a and (u == 2 or not s.scan):
                        rstd(mv_a, ve_a, rs_a, rstd_a, stat_a, 3 * (s.c + 1) + 2, s.c + 1)
                    if s.q and (u == 33 or not s.scan):
                        rstd(mv_q, ve_q, rs_q, rstd_q, res, 1 + 5 * (s.c - 1) + 4, s.c - 1)
                    if s.a and (u == 55 or not s.scan):
                        softplus_series(s)
                    if s.q and (u == UNITS - 1 or not s.scan):
                        scatter(s)

            steps_of(pool.Fori, body)
            pool.wait_ge(slotted, 16 * (ZEROS + TOPK * TJ * NC))

        @block.scalar
        def _(act):
            act.wait_ge(params, 16 * N_PARAMS)
            act.activation(a_neg[:, :, :], a_neg[:, :, :], ACT.Exp).then_inc(neg_set, 1)
            act.wait_ge(neg_set, 1)
            act.mul(a_neg[:, :, :], a_neg[:, :, :], -1.0).then_inc(neg_set, 1)
            act.wait_ge(neg_set, 2)
            act.sem_inc(y_silu, 1)

            def unit(s, u):
                n, db = divmod(u, DB)
                g = s.c * UNITS + u
                if u == 0:
                    act.wait_ge(dt_set, 3 * (s.c + 1))
                wait(act, scan, g - 3)
                act.activation(da[:, u % 4, :], dt[s.par][:, db, :], ACT.Exp, scale=a_neg[:, db, n:n + 1]
                               ).then_inc(da_set, 1)

            def take_xT(s, k):
                act.wait_ge(filled, s.before(f"xT{k}") + 1)
                act.activation(xnT[:, k, :], m_ps[:, :], ACT.Identity, scale=n_w[:, k:k + 1], bias=n_b[:, k:k + 1]
                               ).then_inc(xnT_set, 1)

            def take_in(s, db):
                if db == 0:
                    wait(act, halo, s.c + 1)
                    act.wait_ge(pool_set, 6)
                act.wait_ge(filled, s.before(f"in{db}") + 1)
                act.copy(hin[:, db, KC - 1:KC - 1 + T], m_ps[:, :]).then_inc(hin_set, 1)

            def silu_h(s):
                c = s.c
                act.wait_ge(conv, KC * DB * (c + 2))
                wait(act, y_out, DB * c)
                act.activation(h[1 - s.par][:, :, :], cv[:, :, :], ACT.Silu).then_inc(h_set, 1)

            def softplus(s):
                c, d = s.c, dt[1 - s.par]
                act.wait_ge(z_set, DB * (c + 2))
                wait(act, series, 2 * (c + 1))
                act.activation(ez[:, :, :], z[:, :, :], ACT.Abs).then_inc(soft, 1)
                act.wait_ge(soft, 3 * (c + 1) + 1)
                act.activation(ez[:, :, :], ez[:, :, :], ACT.Exp, scale=-1.0).then_inc(soft, 1)
                act.wait_ge(soft, 3 * (c + 1) + 2)
                act.activation(d[:, :, :], ez[:, :, :], ACT.Ln, bias=1.0).then_inc(soft, 1)

            def silu_y(s):
                act.wait_ge(y_out, DB * s.c)
                act.activation(yv[:, :, :], yv[:, :, :], ACT.Silu).then_inc(y_silu, 1)

            def take_x1T(s, k):
                act.wait_ge(filled, s.before(f"x1T{k}") + 1)
                act.copy(x1T[:, k, :], m_ps[:, :]).then_inc(x1T_set, 1)

            def exp_logits(s):
                act.wait_ge(route, ROUTE * (s.c - 1) + 2)
                act.activation(ex[:, :, :], lg[:, :, :], ACT.Exp).then_inc(e_set, 1)

            def stages(s, u):
                whole = not s.scan
                if s.a and (u == 10 or whole):
                    take_xT(s, 0)
                if s.q and (u == 9 or whole):
                    silu_y(s)
                if s.a and (u == 13 or whole):
                    take_xT(s, 1)
                for db in range(DB):
                    if s.a and (u == 16 + 3 * db or whole):
                        take_in(s, db)
                if s.a and (u == 36 or whole):
                    silu_h(s)
                for k in range(KD):
                    if s.q and (u == 40 + 5 * k or whole):
                        take_x1T(s, k)
                if s.a and (u == 52 or whole):
                    softplus(s)
                if s.q and (u == 53 or whole):
                    exp_logits(s)

            def body(s):
                for u in range(UNITS if s.scan else 1):
                    if s.scan:
                        unit(s, u)
                    stages(s, u)

            steps_of(act.Fori, body)

        @block.vector
        def _(dve):
            dve.wait_ge(params, 16 * N_PARAMS)
            dve.tensor_copy(sel[:, :], sel_raw[:, :]).then_inc(setup, 1)
            dve.sem_inc(res, 1)
            dve.wait_ge(pool_set, 6)

            def mult_b(s, u):
                n, db = divmod(u, DB)
                g = s.c * UNITS + u
                if u == 0:
                    dve.wait_ge(h_set, s.c + 1)
                if db == 0:
                    dve.wait_ge(b_set, NS * s.c + n + 1)
                wait(dve, scan, g - 1)
                dve.tensor_tensor(u_ps[:, u % 2, :], h[s.par][:, db, :], b_ps[:, :], ALU.mult).then_inc(u_set, 1)

            def run_scan(s, u):
                n, db = divmod(u, DB)
                g = s.c * UNITS + u
                dve.wait_ge(u_set, g + 1)
                dve.wait_ge(da_set, g + 1)
                wait(dve, prod_set, g - 7)
                if db == 0:
                    wait(dve, carried, NS * s.c + n - 1)
                dve.tensor_tensor_scan(state[:, n % 2, db, :], da[:, u % 4, :], u_ps[:, u % 2, :],
                                       carry[:, n, db:db + 1], ALU.mult, ALU.add).then_inc(scan, 1)

            def keep_carry(s, n):
                dve.wait_ge(scan, s.c * UNITS + DB * (n + 1))
                dve.tensor_copy(carry[:, n, :], state[:, n % 2, :, T - 1]).then_inc(carried, 1)

            def norm_x(s):
                c = s.c
                dve.wait_ge(x_in, 16 * (c + 2))
                for j in range(TJ):
                    i = dve.bn_stats(st_a[:, j, :], xt[:, j, :])
                i.then_inc(stat_a, 1)
                dve.wait_ge(stat_a, 3 * (c + 1) + 1)
                hold(dve, passed[2])
                for j in range(TJ):
                    i = dve.bn_aggr(mv_a[:, j, :], st_a[:, j, :])
                i.then_inc(stat_a, 1)

            def norm_x_end(s):
                c = s.c
                dve.wait_ge(stat_a, 3 * (c + 1) + 2)
                dve.wait_ge(rstd_a, 2 * (c + 2))
                wait(dve, xnT_set, 2 * (c + 1))
                for j in range(TJ):
                    i = dve.tensor_scalar(xn[:, j, :], xt[:, j, :], mv_a[:, j, 0:1], rs_a[:, j:j + 1],
                                          ALU.subtract, ALU.mult)
                i.then_inc(stat_a, 1)

            def conv_tap(s, db, k):
                c = s.c
                m = KC * DB * (c + 1) + KC * db + k
                w = conv_w[:, db, k:k + 1]
                if k == 0:
                    dve.wait_ge(hin_set, DB * (c + 1) + db + 1)
                    if db == 0:
                        wait(dve, h_set, c + 1)
                    dve.tensor_scalar(cv[:, db, :], hin[:, db, 0:T], w, None, ALU.mult).then_inc(conv, 1)
                else:
                    dve.wait_ge(conv, m)
                    dve.scalar_tensor_tensor(out=cv[:, db, :], in0=hin[:, db, k:k + T], scalar=w, in1=cv[:, db, :],
                                             op0=ALU.mult, op1=ALU.add).then_inc(conv, 1)

            def move_halo(s):
                dve.wait_ge(conv, KC * DB * (s.c + 2))
                dve.tensor_copy(hin[:, :, 0:KC - 1], hin[:, :, T:T + KC - 1]).then_inc(halo, 1)

            def take_bc(s):
                c, o = s.c, 1 - s.par
                dve.wait_ge(filled, s.before("xp") + 1)
                wait(dve, c_out, 16 * (c + 1))
                dve.tensor_copy(bcf[:, :], m_ps[0:2 * NS + 1, :]).then_inc(bc_set, 1)
                dve.wait_ge(bc_set, 3 * (c + 1) + 1)
                wait(dve, b_set, NS * c)
                dve.tensor_copy(bc_hi[o][:, :], bcf[:, :]).then_inc(bc_set, 1)
                dve.wait_ge(bc_set, 3 * (c + 1) + 2)
                dve.tensor_tensor(bc_lo[o][:, :], bcf[:, :], bc_hi[o][:, :].bitcast(F32), ALU.subtract
                                  ).then_inc(bc_set, 1)

            def take_dt(s):
                c = s.c
                dve.wait_ge(filled, s.before("dtb") + 1)
                wait(dve, soft, 3 * (c + 1))
                wait(dve, dt_set, 3 * (c + 1))
                for db in range(DB):
                    i = dve.tensor_scalar(z[:, db, :], m_ps[:, :], dt_w[:, db:db + 1], dt_b[:, db:db + 1],
                                          ALU.mult, ALU.add).then_inc(z_set, 1)

            def finish_dt(s):
                c, d = s.c, dt[1 - s.par]
                dve.wait_ge(soft, 3 * (c + 2))
                dve.tensor_scalar(small[:, :, :], ez[:, :, :], TINY, None, ALU.is_lt).then_inc(dt_set, 1)
                dve.wait_ge(dt_set, 3 * (c + 1) + 1)
                dve.wait_ge(series, 2 * (c + 2))
                hold(dve, passed[2])
                dve.copy_predicated(d[:, :, :], small[:, :, :], ser[:, :, :]).then_inc(dt_set, 1)
                dve.wait_ge(dt_set, 3 * (c + 1) + 2)
                dve.scalar_tensor_tensor(out=d[:, :, :].rearrange("p a b -> p (a b)"),
                                         in0=z[:, :, :].rearrange("p a b -> p (a b)"), scalar=0.0,
                                         in1=d[:, :, :].rearrange("p a b -> p (a b)"),
                                         op0=ALU.max, op1=ALU.add).then_inc(dt_set, 1)

            def take_y(s, db):
                dve.wait_ge(summed, s.c * UNITS)
                if db == 0:
                    wait(dve, y_silu, s.c)
                dve.scalar_tensor_tensor(out=yv[:, db, :], in0=h[1 - s.par][:, db, :], scalar=d_skip[:, db:db + 1],
                                         in1=y_ps[:, db, :], op0=ALU.mult, op1=ALU.add).then_inc(y_out, 1)

            def residual(s, half):
                k = 1 + 5 * (s.c - 1)
                dve.wait_ge(filled, s.before(f"op{half}") + 1)
                if half == 0:
                    dve.wait_ge(xr_in, 16 * s.c)
                r = xr[:, 2 * half:2 * half + 2, :].rearrange("p a b -> p (a b)")
                dve.scalar_tensor_tensor(out=r, in0=r, scalar=2.0, in1=m_ps[:, :], op0=ALU.mult, op1=ALU.add
                                         ).then_inc(res, 1)
                dve.wait_ge(res, k + half + 1)

            def stats_q(s):
                k = 1 + 5 * (s.c - 1)
                for j in range(TJ):
                    i = dve.bn_stats(st_q[:, j, :], xr[:, j, :])
                i.then_inc(res, 1)
                dve.wait_ge(res, k + 3)
                hold(dve, passed[2])
                for j in range(TJ):
                    i = dve.bn_aggr(mv_q[:, j, :], st_q[:, j, :])
                i.then_inc(res, 1)

            def norm_q(s):
                c = s.c
                dve.wait_ge(res, 1 + 5 * (c - 1) + 4)
                dve.wait_ge(rstd_q, 2 * c)
                dve.wait_ge(x1_out, 1 + 16 * (c - 1))
                dve.wait_ge(slotted, 16 * (ZEROS + TOPK * TJ * (c - 1)))
                for j in range(TJ):
                    i = dve.tensor_scalar(x1[:, j, :], xr[:, j, :], mv_q[:, j, 0:1], rs_q[:, j:j + 1],
                                          ALU.subtract, ALU.mult)
                i.then_inc(res, 1)

            def over_e(a):
                return a.unsqueeze(2).to_broadcast([P, TJ, E])

            def routing(s, part):
                c = s.c
                n = [{0: 0, 1: 2, 2: 20}[part]]
                r0 = ROUTE * (c - 1)

                def done(i):
                    n[0] += 1
                    i.then_inc(route, 1)
                    dve.wait_ge(route, r0 + n[0])

                if part == 0:
                    dve.wait_ge(filled, s.before("rt") + 1)
                    logits = m_ps[:, 0:TJ * E].rearrange("p (j e) -> p j e", e=E)
                    done(dve.tensor_reduce(mx[:, :], logits, AX.X, ALU.max))
                    done(dve.tensor_tensor(lg[:, :, :], logits, over_e(mx[:, :]), ALU.subtract))
                if part == 1:
                    dve.wait_ge(e_set, c)
                    done(dve.tensor_reduce(su[:, :], ex[:, :, :], AX.X, ALU.add))
                    done(dve.reciprocal(rsu[:, :], su[:, :]))
                    done(dve.tensor_tensor(pr[:, :, :], ex[:, :, :], over_e(rsu[:, :]), ALU.mult))
                    src = pr
                    for k in range(TOPK):
                        done(dve.tensor_reduce(pk[:, k, :], src[:, :, :], AX.X, ALU.max))
                        done(dve.tensor_tensor(eq[:, :, :], src[:, :, :], over_e(pk[:, k, :]), ALU.is_equal))
                        done(dve.tensor_tensor(wr[:, :, :], eq[:, :, :], rank, ALU.mult))
                        done(dve.tensor_reduce(wm[:, :], wr[:, :, :], AX.X, ALU.max))
                        done(dve.tensor_tensor(oh[:, k, :, :], wr[:, :, :], over_e(wm[:, :]), ALU.is_equal))
                        if k == 0:
                            done(dve.scalar_tensor_tensor(
                                out=pr2[:, :, :].rearrange("p a b -> p (a b)"),
                                in0=oh[:, 0, :, :].rearrange("p a b -> p (a b)"), scalar=-2.0,
                                in1=pr[:, :, :].rearrange("p a b -> p (a b)"), op0=ALU.mult, op1=ALU.add))
                            src = pr2
                    done(dve.tensor_tensor(hot_before[:, :], hot_before[:, :], hot_sum[:, :], ALU.add))
                    done(dve.tensor_tensor(hot[:, :, :], oh[:, 0, :, :], oh[:, 1, :, :], ALU.add))
                    done(dve.tensor_reduce(hot_sum[:, :], hot[:, :, :].rearrange("p j e -> p e j"), AX.X, ALU.add))
                    done(dve.tensor_tensor(den[:, :], pk[:, 0, :], pk[:, 1, :], ALU.add))
                if part == 2:
                    posn = m_ps[:, 0:TJ * E].rearrange("p (j e) -> p j e", e=E)
                    ohf = oh[:, :, :, :].rearrange("p k j e -> p (k j) e")
                    dve.wait_ge(filled, s.before("pos") + 1)
                    done(dve.tensor_tensor(po[:, 0:TJ, :], oh[:, 0, :, :], posn, ALU.mult))
                    done(dve.tensor_tensor(po[:, TJ:2 * TJ, :], oh[:, 1, :, :], posn, ALU.mult))
                    done(dve.tensor_reduce(pos_k[:, :], po[:, :, :], AX.X, ALU.add))
                    done(dve.tensor_tensor(bo[:, :, :], ohf, base8, ALU.mult))
                    done(dve.tensor_reduce(base_k[:, :], bo[:, :, :], AX.X, ALU.add))
                    done(dve.tensor_scalar(keep[:, :], pos_k[:, :], float(CAP), None, ALU.is_lt))
                    done(dve.reciprocal(rden[:, :], den[:, :]))
                    done(dve.tensor_tensor(gk[:, :, :], pk[:, :, :],
                                           rden[:, :].unsqueeze(1).to_broadcast([P, TOPK, TJ]), ALU.mult))
                    done(dve.tensor_tensor(gates[:, bass.ds((c - 1) * 8, 8)], gk[:, :, :].rearrange("p k j -> p (k j)"),
                                           keep[:, :], ALU.mult))
                    done(dve.tensor_tensor(kpos[:, :], keep[:, :], pos_k[:, :], ALU.mult))
                    done(dve.tensor_tensor(slot_of[:, bass.ds((c - 1) * 8, 8)], kpos[:, :], base_k[:, :], ALU.add))
                    trash = cst[:, bass.ds((c - 1) * 8 + C_TRASH, 8)]
                    done(dve.tensor_tensor(kpos[:, :], kpos[:, :], base_k[:, :], ALU.add))
                    done(dve.tensor_tensor(far[:, :], kpos[:, :], trash, ALU.subtract))
                    done(dve.tensor_tensor(far[:, :], far[:, :], keep[:, :], ALU.mult))
                    done(dve.tensor_tensor(sidx[:, :], far[:, :], trash, ALU.add))
                    assert n[0] == ROUTE

            def stages(s, u):
                whole = not s.scan
                if s.a and (u == 0 or whole):
                    norm_x(s)
                if s.a and (u == 4 or whole):
                    norm_x_end(s)
                for db in range(DB):
                    if s.q and (u == 3 + db or whole):
                        take_y(s, db)
                for db in range(DB):
                    for k in range(KC):
                        if s.a and (u == 18 + 4 * db + k or whole):
                            conv_tap(s, db, k)
                if s.a and (u == 34 or whole):
                    move_halo(s)
                for half in range(2):
                    if s.q and (u == 28 + 3 * half or whole):
                        residual(s, half)
                if s.q and (u == 31 or whole):
                    stats_q(s)
                if s.q and (u == 35 or whole):
                    norm_q(s)
                if s.a and (u == 42 or whole):
                    take_bc(s)
                if s.a and (u == 47 or whole):
                    take_dt(s)
                if s.q and (u == 50 or whole):
                    routing(s, 0)
                if s.q and (u == 54 or whole):
                    routing(s, 1)
                if s.a and (u == 61 or whole):
                    finish_dt(s)
                if s.q and (u == 59 or whole):
                    routing(s, 2)

            def body(s):
                if not s.scan:
                    stages(s, 0)
                    return
                mult_b(s, 0)
                for u in range(UNITS):
                    if u + 1 < UNITS:
                        mult_b(s, u + 1)
                    run_scan(s, u)
                    if u % DB == 1 and u > DB:
                        keep_carry(s, u // DB - 1)
                    stages(s, u)
                keep_carry(s, NS - 1)

            steps_of(dve.Fori, body)

        @block.tensor
        def _(pe):
            pe.wait_ge(params, 16 * N_PARAMS)
            pe.wait_ge(setup, 1)

            def spread_b(c, par, n):
                if n == 0:
                    pe.wait_ge(bc_set, 3 * (c + 1))
                wait(pe, u_set, c * UNITS + DB * n)
                pe.matmul(b_ps[:, :], sel[:, (n + 1) * P:(n + 2) * P], bc_hi[par][:, :], start=True, stop=False)
                pe.matmul(b_ps[:, :], sel[:, (n + 1) * P:(n + 2) * P], bc_lo[par][:, :], start=False, stop=True
                          ).then_inc(b_set, 1)

            def add_up(s, u):
                n, db = divmod(u, DB)
                pe.wait_ge(prod_set, s.c * UNITS + u + 1)
                if u < DB:
                    wait(pe, y_out, DB * (s.c - 1) + db + 1)
                pe.matmul(y_ps[:, db, :], ident, prod[:, u % 4, :], start=(n == 0), stop=(n == NS - 1)
                          ).then_inc(summed, 1)

            def read(use, c):
                k = int(use[-1]) if use[-1].isdigit() else 0
                return {"xT": (xnT_set, KD * (c + 1) + k + 1), "in": (hin_set, DB * (c + 1) + k + 1),
                        "op": (res, 1 + 5 * (c - 1) + k + 1), "x1T": (x1T_set, KD * (c - 1) + k + 1),
                        "xp": (bc_set, 3 * (c + 1) + 1), "dtb": (z_set, DB * (c + 2)),
                        "rt": (route, ROUTE * (c - 1) + 2), "pos": (route, ROUTE * (c - 1) + 22)
                        }[use.rstrip("0123456789")]

            def take_bank(s, use):
                i = s.uses.index(use)
                if i > 0:
                    pe.wait_ge(*read(s.uses[i - 1], s.c))
                elif use != "xT0":
                    pe.wait_ge(*read("pos", s.c - 1))

            def xT(s, k):
                if k == 0:
                    pe.wait_ge(stat_a, 3 * (s.c + 2))
                take_bank(s, f"xT{k}")
                for j in range(TJ):
                    i = pe.transpose(m_ps[:, j * P:(j + 1) * P], xn[:, j, k * P:(k + 1) * P], ident)
                i.then_inc(filled, 1)

            def in_proj(s, db):
                if db == 0:
                    pe.wait_ge(xnT_set, 2 * (s.c + 2))
                take_bank(s, f"in{db}")
                for k in range(KD):
                    i = pe.matmul(m_ps[:, :], w_in[:, k, db * P:(db + 1) * P], xnT[:, k, :],
                                  start=(k == 0), stop=(k == KD - 1))
                i.then_inc(filled, 1)

            def x_proj(s):
                pe.wait_ge(h_set, s.c + 2)
                take_bank(s, "xp")
                for db in range(DB):
                    i = pe.matmul(m_ps[0:2 * NS + 1, :], w_x[:, db, :], h[1 - s.par][:, db, :],
                                  start=(db == 0), stop=(db == DB - 1))
                i.then_inc(filled, 1)

            def spread_dt(s):
                pe.wait_ge(bc_set, 3 * (s.c + 2))
                take_bank(s, "dtb")
                pe.matmul(m_ps[:, :], sel[:, 0:P], bc_hi[1 - s.par][:, :], start=True, stop=False)
                pe.matmul(m_ps[:, :], sel[:, 0:P], bc_lo[1 - s.par][:, :], start=False, stop=True).then_inc(filled, 1)

            def out_proj(s, half):
                if half == 0:
                    pe.wait_ge(y_silu, 1 + s.c)
                take_bank(s, f"op{half}")
                for jj in range(2):
                    j = 2 * half + jj
                    for db in range(DB):
                        i = pe.matmul(m_ps[:, jj * D:(jj + 1) * D], yv[:, db, j * P:(j + 1) * P], w_out[:, db, :],
                                      start=(db == 0), stop=(db == DB - 1))
                i.then_inc(filled, 1)

            def x1_T(s, k):
                if k == 0:
                    pe.wait_ge(res, 1 + 5 * s.c)
                take_bank(s, f"x1T{k}")
                for j in range(TJ):
                    i = pe.transpose(m_ps[:, j * P:(j + 1) * P], x1[:, j, k * P:(k + 1) * P], ident)
                i.then_inc(filled, 1)

            def router(s):
                pe.wait_ge(x1T_set, 2 * s.c)
                take_bank(s, "rt")
                for j in range(TJ):
                    for k in range(KD):
                        i = pe.matmul(m_ps[:, j * E:(j + 1) * E], x1T[:, k, j * P:(j + 1) * P], w_r[:, k, :],
                                      start=(k == 0), stop=(k == KD - 1))
                i.then_inc(filled, 1)

            def positions(s):
                pe.wait_ge(route, ROUTE * (s.c - 1) + 20)
                take_bank(s, "pos")
                for j in range(TJ):
                    o = m_ps[:, j * E:(j + 1) * E]
                    pe.matmul(o, tri, hot[:, j, :], start=True, stop=False)
                    for i in range(j):
                        pe.matmul(o, ones, hot[:, i, :], start=False, stop=False)
                    last = pe.matmul(o, ones, hot_before[:, :], start=False, stop=True)
                last.then_inc(filled, 1)

            def stages(s, u):
                whole = not s.scan
                if s.a and (u == 6 or whole):
                    xT(s, 0)
                if s.a and (u == 9 or whole):
                    xT(s, 1)
                for db in range(DB):
                    if s.a and (u == 12 + 3 * db or whole):
                        in_proj(s, db)
                for half in range(2):
                    if s.q and (u == 24 + 3 * half or whole):
                        out_proj(s, half)
                if s.q and (u == 36 or whole):
                    x1_T(s, 0)
                if s.a and (u == 38 or whole):
                    x_proj(s)
                if s.q and (u == 41 or whole):
                    x1_T(s, 1)
                if s.a and (u == 43 or whole):
                    spread_dt(s)
                if s.q and (u == 46 or whole):
                    router(s)
                if s.q and (u == 55 or whole):
                    positions(s)

            def body(s):
                if not s.scan:
                    stages(s, 0)
                    if s.a:
                        spread_b(0, 0, 0)
                    return
                for u in range(UNITS):
                    if u % DB == 0 and u + DB < UNITS:
                        spread_b(s.c, s.par, u // DB + 1)
                    if u == UNITS - DB and s.a:
                        spread_b(s.c + 1, 1 - s.par, 0)
                    add_up(s, u)
                    stages(s, u)

            steps_of(pe.Fori, body)


def experts(nc, io, scr):
    with ExitStack() as ctx:
        def sb(name, shape, dt=F32):
            return ctx.enter_context(nc.sbuf_tensor(name, shape, dt))

        def sem(name):
            return ctx.enter_context(nc.semaphore(name))

        HALF = CAP // 2
        PASSES = ((0, 0), (0, 1), (1, 0))
        XG = KD * CT // 4
        HG = 2 * HB

        ident = sb("ident2", [P, P])
        b1 = sb("b1", [P, HB, E])
        b2 = sb("b2", [P, E, D])
        rows = [sb(f"rows{i}", [P, CT, D]) for i in range(2)]
        xT = [sb(f"xT_{n}", [P, KD * CAP], F32R) for n in ("hi", "lo")]
        w1_raw = sb("w1_raw", [P, KD, H])
        w2_raw = sb("w2_raw", [P, HB, D])
        w1 = [[sb(f"w1_{n}{i}", [P, KD, H], F32R) for n in ("hi", "lo")] for i in range(2)]
        w2 = [[sb(f"w2_{n}{i}", [P, HB, D], F32R) for n in ("hi", "lo")] for i in range(2)]
        b1_e = sb("b1_e", [P, 2, HB])
        relu = sb("relu", [P, 4, HALF])
        hid = [sb(f"hid_{n}", [P, HB, CAP], F32R) for n in ("hi", "lo")]
        eo = sb("eo", [P, CT, D])
        x_ps = ctx.enter_context(nc.psum_tensor("x_ps", [P, 2, 512], F32))
        h_ps = ctx.enter_context(nc.psum_tensor("h_ps", [P, 4, 512], F32))
        o_ps = ctx.enter_context(nc.psum_tensor("o_ps", [P, 2, 512], F32))

        params = sem("params2")
        rows_in = [sem("rows_in0"), sem("rows_in1")]
        w_in = sem("w_in2")
        b1_set = sem("b1_set")
        w_hi = sem("w_hi")
        w_lo = sem("w_lo")
        x_tr = sem("x_tr")
        x_hi = sem("x_hi")
        x_lo = sem("x_lo")
        h_mm = sem("h_mm")
        h_relu = sem("h_relu")
        h_hi = sem("h_hi")
        h_lo = [sem("h_lo_even"), sem("h_lo_odd")]
        o_mm = sem("o_mm")
        o_set = sem("o_set")
        o_out = sem("o_out")

        block = ctx.enter_context(nc.Block())

        def over_experts(engine_loop, body):
            body(0, 0, True)
            with engine_loop(1, E - 2, 2) as e:
                body(e, 1, True)
                body(e + 1, 0, True)
            body(E - 1, 1, False)

        @block.sync
        def _(sp):
            sp.dma_start(ident[:, :], io["consts"][:, C_ID:C_ID + P]).then_inc(params, 16)
            sp.dma_start(b1[:, :, :], io["b1"]).then_inc(params, 16)
            sp.dma_start(b2[:, :, :], io["b2"].partition_broadcast(P)).then_inc(params, 16)

            def load(e, par):
                wait(sp, x_tr, XG * (e - 1))
                sp.dma_start(rows[par][:, :, :], scr["expert_in"][bass.ds(e * CAP, CAP), :]
                             .rearrange("(j p) d -> p j d", p=P)).then_inc(rows_in[par], 16)
                wait(sp, w_lo, 2 * e)
                sp.dma_start(w1_raw[:, :, :], io["w1"][bass.ds(e * D, D), :].rearrange("(k p) n -> p k n", p=P)
                             ).then_inc(w_in, 16)
                sp.dma_start(w2_raw[:, :, :], io["w2"][bass.ds(e * H, H), :].rearrange("(k p) n -> p k n", p=P)
                             ).then_inc(w_in, 16)

            def body(e, par, more):
                if more:
                    load(e + 1, 1 - par)
                for half in range(2):
                    sp.wait_ge(o_set, CT * e + 3 * (half + 1))
                    sp.dma_start(scr["expert_out"][bass.ds(e * CAP + half * HALF, HALF), :]
                                 .rearrange("(j p) d -> p j d", p=P), eo[:, 3 * half:3 * half + 3, :]
                                 ).then_inc(o_out, 16)

            load(0, 0)
            over_experts(sp.Fori, body)
            sp.wait_ge(o_out, 32 * E)

        @block.gpsimd
        def _(pool):
            def split_weights(e, par):
                for k, (w, raw) in enumerate(((w1, w1_raw), (w2, w2_raw))):
                    pool.wait_ge(w_hi, 2 * e + k + 1)
                    pool.tensor_tensor(w[par][1][:, :, :], raw[:, :, :], w[par][0][:, :, :].bitcast(F32), ALU.subtract
                                       ).then_inc(w_lo, 1)

            def body(e, par, more):
                for hb in range(HB):
                    pool.wait_ge(h_hi, HG * e + 2 * hb + 1)
                    pool.tensor_tensor(hid[1][:, hb, 0:HALF], relu[:, 2 * hb % 4, :],
                                       hid[0][:, hb, 0:HALF].bitcast(F32), ALU.subtract).then_inc(h_lo[0], 1)
                if more:
                    split_weights(e + 1, 1 - par)

            split_weights(0, 0)
            over_experts(pool.Fori, body)

        @block.scalar
        def _(act):
            act.wait_ge(params, 48)

            def high_weights(e, par, k):
                if k == 0:
                    act.wait_ge(w_in, 32 * (e + 1))
                    wait(act, o_mm, CT * (e - 1))
                w, raw = ((w1, w1_raw), (w2, w2_raw))[k]
                act.copy(w[par][0][:, :, :], raw[:, :, :]).then_inc(w_hi, 1)

            def high_x(e, par):
                wait(act, h_mm, HG * e)
                for g in range(XG):
                    act.wait_ge(x_tr, XG * e + g + 1)
                    act.copy(xT[0][:, g * 512:(g + 1) * 512], x_ps[:, (par + g) % 2, :]).then_inc(x_hi, 1)

            def body(e, par, more):
                act.copy(b1_e[:, par, :], b1[:, :, bass.ds(e, 1)].rearrange("p h o -> p (h o)")).then_inc(b1_set, 1)
                act.wait_ge(b1_set, e + 1)
                for g in range(HG):
                    hb, half = divmod(g, 2)
                    act.wait_ge(h_mm, HG * e + g + 1)
                    wait(act, h_lo[half], HB * e + hb - 1)
                    act.activation(relu[:, g % 4, :], h_ps[:, g % 4, 0:HALF], ACT.Relu, bias=b1_e[:, par, hb:hb + 1]
                                   ).then_inc(h_relu, 1)
                    if more and g in (3, 9):
                        high_weights(e + 1, 1 - par, g // 9)
                if more:
                    high_x(e + 1, 1 - par)

            high_weights(0, 0, 0)
            high_weights(0, 0, 1)
            high_x(0, 0)
            over_experts(act.Fori, body)

        @block.vector
        def _(dve):
            dve.wait_ge(params, 48)

            def low_x(e, par):
                wait(dve, h_mm, HG * e)
                for g in range(XG):
                    cols = slice(g * 512, (g + 1) * 512)
                    dve.wait_ge(x_hi, XG * e + g + 1)
                    dve.tensor_tensor(xT[1][:, cols], x_ps[:, (par + g) % 2, :], xT[0][:, cols].bitcast(F32),
                                      ALU.subtract).then_inc(x_lo, 1)

            def body(e, par, more):
                wait(dve, o_mm, CT * e)
                for g in range(HG):
                    hb, half = divmod(g, 2)
                    cols = slice(half * HALF, (half + 1) * HALF)
                    dve.wait_ge(h_relu, HG * e + g + 1)
                    dve.tensor_copy(hid[0][:, hb, cols], relu[:, g % 4, :]).then_inc(h_hi, 1)
                    if half == 1:
                        dve.wait_ge(h_hi, HG * e + g + 1)
                        dve.tensor_tensor(hid[1][:, hb, cols], relu[:, g % 4, :], hid[0][:, hb, cols].bitcast(F32),
                                          ALU.subtract).then_inc(h_lo[1], 1)
                if more:
                    low_x(e + 1, 1 - par)
                for j in range(CT):
                    dve.wait_ge(o_mm, CT * e + j + 1)
                    if j % 3 == 0:
                        wait(dve, o_out, 32 * e)
                    dve.tensor_tensor(eo[:, j, :], o_ps[:, j % 2, 0:D],
                                      b2[:, bass.ds(e, 1), :].rearrange("p o d -> p (o d)"), ALU.add).then_inc(o_set, 1)

            low_x(0, 0)
            over_experts(dve.Fori, body)

        @block.tensor
        def _(pe):
            pe.wait_ge(params, 48)

            def turn(e, par):
                pe.wait_ge(rows_in[par], 8 * (e - par) + 16)
                for g in range(XG):
                    wait(pe, x_lo, XG * e + g - 1)
                    for i in range(4):
                        k, j = divmod(4 * g + i, CT)
                        last = pe.transpose(x_ps[:, (par + g) % 2, i * P:(i + 1) * P], rows[par][:, j, k * P:(k + 1) * P],
                                            ident[:, :])
                    last.then_inc(x_tr, 1)

            def hidden(e, par):
                pe.wait_ge(x_lo, XG * (e + 1))
                pe.wait_ge(w_lo, 2 * e + 1)
                for g in range(HG):
                    hb, half = divmod(g, 2)
                    wait(pe, h_relu, HG * e + g - 3)
                    n = 0
                    for a, b in PASSES:
                        for k in range(KD):
                            c0 = k * CAP + half * HALF
                            last = pe.matmul(h_ps[:, g % 4, 0:HALF], w1[par][a][:, k, hb * P:(hb + 1) * P],
                                             xT[b][:, c0:c0 + HALF], start=(n == 0), stop=(n == 3 * KD - 1))
                            n += 1
                    last.then_inc(h_mm, 1)

            def outputs(e, par):
                pe.wait_ge(h_lo[0], HB * (e + 1))
                pe.wait_ge(h_lo[1], HB * (e + 1))
                pe.wait_ge(w_lo, 2 * e + 2)
                for j in range(CT):
                    wait(pe, o_set, CT * e + j - 1)
                    n = 0
                    for a, b in PASSES:
                        for hb in range(HB):
                            last = pe.matmul(o_ps[:, j % 2, 0:D], hid[a][:, hb, j * P:(j + 1) * P], w2[par][b][:, hb, :],
                                             start=(n == 0), stop=(n == 3 * HB - 1))
                            n += 1
                    last.then_inc(o_mm, 1)

            def body(e, par, more):
                hidden(e, par)
                if more:
                    turn(e + 1, 1 - par)
                outputs(e, par)

            turn(0, 0)
            over_experts(pe.Fori, body)


def combine(nc, scr, gates, slot_of, out):
    with ExitStack() as ctx:
        def sb(name, shape, dt=F32):
            return ctx.enter_context(nc.sbuf_tensor(name, shape, dt))

        def sem(name):
            return ctx.enter_context(nc.semaphore(name))

        got = sb("got", [P, NC, TOPK, TJ, D])
        x1 = sb("x1_all", [P, NC, TJ, D])
        st = sb("st_f", [P, NC, TJ, 6])
        mv = sb("mv_f", [P, NC, TJ, 2])
        ve = sb("ve_f", [P, NC, TJ])
        sd = sb("sd_f", [P, NC, TJ])
        rs = sb("rs_f", [P, NC, TJ])

        rows_in = [sem(f"got{c}") for c in range(NC)]
        x1_in = [sem(f"x1_in{c}") for c in range(NC)]
        mixed = sem("mixed")
        rooted = sem("rooted")
        normed = sem("normed")
        stored = sem("stored")

        block = ctx.enter_context(nc.Block())

        @block.gpsimd
        def _(pool):
            for c in range(NC):
                for k in range(TOPK):
                    for j in range(TJ):
                        col = (c * TOPK + k) * TJ + j
                        pool.indirect_dma_start(got[:, c, k, j, :], None, scr["expert_out"],
                                                bass.IndirectOffsetOnAxis(slot_of[:, col:col + 1], 0)
                                                ).then_inc(rows_in[c], 16)

        @block.sync
        def _(sp):
            for c in range(NC):
                sp.dma_start(x1[:, c, :, :], scr["x1"][c * T:(c + 1) * T, :].rearrange("(j p) d -> p j d", p=P)
                             ).then_inc(x1_in[c], 16)
            with sp.Fori(0, NC) as c:
                sp.wait_ge(normed, 2 * c + 2)
                sp.dma_start(out[bass.ds(c * T, T), :].rearrange("(j p) d -> p j d", p=P),
                             x1[:, bass.ds(c, 1), :, :].rearrange("p o j d -> p (o j) d")).then_inc(stored, 16)
            sp.wait_ge(stored, 16 * NC)

        @block.scalar
        def _(act):
            with act.Fori(0, NC) as c:
                act.wait_ge(mixed, 5 * c + 5)
                act.activation(sd[:, bass.ds(c, 1), :], ve[:, bass.ds(c, 1), :], ACT.Sqrt).then_inc(rooted, 1)

        @block.vector
        def _(dve):
            def mix(c):
                dve.wait_ge(rows_in[c], 16 * TOPK * TJ)
                dve.wait_ge(x1_in[c], 16)
                for k in range(TOPK):
                    for j in range(TJ):
                        col = (c * TOPK + k) * TJ + j
                        i = dve.scalar_tensor_tensor(out=x1[:, c, j, :], in0=got[:, c, k, j, :],
                                                     scalar=gates[:, col:col + 1], in1=x1[:, c, j, :],
                                                     op0=ALU.mult, op1=ALU.add)
                    i.then_inc(mixed, 1)
                    dve.wait_ge(mixed, 5 * c + k + 1)
                for j in range(TJ):
                    i = dve.bn_stats(st[:, c, j, :], x1[:, c, j, :])
                i.then_inc(mixed, 1)
                dve.wait_ge(mixed, 5 * c + 3)
                for j in range(TJ):
                    i = dve.bn_aggr(mv[:, c, j, :], st[:, c, j, :])
                i.then_inc(mixed, 1)
                dve.wait_ge(mixed, 5 * c + 4)
                dve.tensor_scalar(ve[:, c, :], mv[:, c, :, 1], EPS, None, ALU.add).then_inc(mixed, 1)

            def norm(c):
                dve.wait_ge(rooted, c + 1)
                dve.reciprocal(rs[:, c, :], sd[:, c, :]).then_inc(normed, 1)
                dve.wait_ge(normed, 2 * c + 1)
                for j in range(TJ):
                    i = dve.tensor_scalar(x1[:, c, j, :], x1[:, c, j, :], mv[:, c, j, 0:1], rs[:, c, j:j + 1],
                                          ALU.subtract, ALU.mult)
                i.then_inc(normed, 1)

            for c in range(NC):
                mix(c)
                if c > 0:
                    norm(c - 1)
            norm(NC - 1)


def program(nc, io, out):
    scr = {
        "expert_in": nc.dram_tensor("expert_in", (SLOTS + TOPK * L, D), F32, kind="Internal").ap(),
        "expert_out": nc.dram_tensor("expert_out", (SLOTS, D), F32, kind="Internal").ap(),
        "x1": nc.dram_tensor("x1_scratch", (L, D), F32, kind="Internal").ap(),
        "c": nc.dram_tensor("c_scratch", (NS, L), F32, kind="Internal").ap(),
    }
    cols = TOPK * L // P
    with nc.sbuf_tensor("gates", [P, cols], F32) as gates, nc.sbuf_tensor("slot_of", [P, cols], U32) as slot_of:
        mixer_and_routing(nc, io, scr, gates, slot_of)
        experts(nc, io, scr)
        combine(nc, scr, gates, slot_of, out)


def constants():
    import numpy as np

    c = np.zeros((P, C_END), np.float32)
    c[:, C_ID:C_ID + P] = np.eye(P)
    c[:, C_TRI:C_TRI + P] = np.triu(np.ones((P, P)), 1)
    c[:, C_ONE:C_ONE + P] = 1
    c[:, C_RANK:C_RANK + TJ * E] = np.tile(E - np.arange(E), TJ)
    c[:, C_BASE:C_BASE + TOPK * TJ * E] = np.tile(CAP * np.arange(E), TOPK * TJ)
    for ch in range(NC):
        for k in range(TOPK):
            for j in range(TJ):
                t = ch * T + j * P + np.arange(P)
                c[:, C_TRASH + (ch * TOPK + k) * TJ + j] = SLOTS + TOPK * t + k
    sel = np.zeros((2 * NS + 1, NS + 1, P), np.float32)
    for n in range(NS + 1):
        sel[n, n, :] = 1
    return c, sel.reshape(2 * NS + 1, (NS + 1) * P)


def kernel(**inputs):
    import numpy as np
    import concourse.bacc as bacc
    from concourse.bass_utils import run_bass_kernel_spmd

    a = {k.split("_", 2)[2]: np.asarray(v) for k, v in inputs.items() if k.startswith("L0_attn_")}
    f = {k.split("_", 2)[2]: np.asarray(v) for k, v in inputs.items() if k.startswith("L0_ffn_")}
    consts, sel = constants()
    by_block = lambda v: np.ascontiguousarray(v.reshape(-1, P).T)
    arrays = {
        "x": a["x"].reshape(L, D), "w_in": a["in_proj_w"].T, "w_out": a["out_proj_w"].T, "w_x": a["x_proj_w"].T,
        "w_router": f["w_router"], "a_log": a["A_log"], "conv_w": a["conv_w"], "dt_w": by_block(a["dt_proj_w"]),
        "dt_b": by_block(a["dt_proj_b"]), "d_skip": by_block(a["D"]), "n_w": by_block(a["norm_w"]),
        "n_b": by_block(a["norm_b"]), "w1": f["w1"].reshape(E * D, H), "w2": f["w2"].reshape(E * H, D),
        "b1": f["b1"].reshape(E, HB, P).transpose(2, 1, 0), "b2": f["b2"], "consts": consts, "sel": sel,
    }
    nc = bacc.Bacc("TRN2", target_bir_lowering=False, num_devices=1)
    arrays = {f"in_{k}": np.ascontiguousarray(v) for k, v in arrays.items()}
    io = {k[3:]: nc.dram_tensor(k, v.shape, mybir.dt.from_np(v.dtype), kind="ExternalInput").ap()
          for k, v in arrays.items()}
    out = nc.dram_tensor("out", (L, D), F32, kind="ExternalOutput").ap()
    program(nc, io, out)
    r = run_bass_kernel_spmd(nc, [arrays], core_ids=[0])
    return r.results[0]["out"].reshape(1, L, D)
```

```python
from contextlib import ExitStack

import concourse.bass as bass
from concourse import mybir

F32 = mybir.dt.float32
F32R = mybir.dt.float32r
U32 = mybir.dt.uint32
U8 = mybir.dt.uint8
ALU = mybir.AluOpType
ACT = mybir.ActivationFunctionType
AX = mybir.AxisListType

P = 128
L = 4096
D = 256
DI = 512
NS = 16
KC = 4
T = 512
NC = L // T
TJ = T // P
DB = DI // P
KD = D // P
UNITS = NS * DB
DA = 8
XB = 4
E = 8
H = 1024
HB = H // P
TOPK = 2
CAP = int(1.5 * 4 * 512 * TOPK / E)
CT = CAP // P
SLOTS = E * CAP
EPS = 1e-5
ROUTE = 35
ZEROS = SLOTS * D // (P * 1024)
N_PARAMS = 12
TINY = 2.0 ** -8

C_ID, C_TRI, C_ONE, C_RANK, C_BASE, C_TRASH, C_END = 0, 128, 256, 384, 416, 480, 544

A_USES = ["xT0", "xT1", "in0", "in1", "in2", "in3", "hT0", "hT1", "hT2", "hT3", "pT", "rows", "dt"]
Q_USES = ["op0", "op1", "x1T0", "x1T1", "rt", "pos"]


class Step:

    def __init__(self, c, par, a=True, scan=True, q=True):
        self.c, self.par, self.a, self.scan, self.q = c, par, a, scan, q

    def a_count(self, use):
        return len(A_USES) * (self.c + 1) + A_USES.index(use) + 1

    def q_count(self, use):
        return len(Q_USES) * (self.c - 1) + Q_USES.index(use) + 1


def steps_of(engine_loop, body):
    body(Step(-1, 1, scan=False, q=False))
    body(Step(0, 0, q=False))
    with engine_loop(1, NC - 2, 2) as c:
        body(Step(c, 1))
        body(Step(c + 1, 0))
    body(Step(NC - 1, (NC - 1) % 2, a=False))
    body(Step(NC, NC % 2, a=False, scan=False))


def wait(eng, sem, value):
    if not isinstance(value, int) or value > 0:
        eng.wait_ge(sem, value)


def hold(eng, passed):
    eng.sem_inc(passed, 1)


def mixer_and_routing(nc, io, scr, gates, slot_of):
    with ExitStack() as ctx:
        def sb(name, shape, dt=F32):
            return ctx.enter_context(nc.sbuf_tensor(name, shape, dt))

        def ps(name, shape):
            return ctx.enter_context(nc.psum_tensor(name, shape, F32))

        def sem(name):
            return ctx.enter_context(nc.semaphore(name))

        cst = sb("cst", [P, C_END])
        ident, tri, ones = cst[:, C_ID:C_ID + P], cst[:, C_TRI:C_TRI + P], cst[:, C_ONE:C_ONE + P]
        rank = cst[:, C_RANK:C_RANK + 32].rearrange("p (j e) -> p j e", e=E)
        base8 = cst[:, C_BASE:C_BASE + 64].rearrange("p (k e) -> p k e", e=E)
        w_in = sb("w_in", [P, KD, DI])
        w_out = sb("w_out", [P, DB, D])
        w_x = sb("w_x", [P, DB, 2 * NS + 1])
        w_r = sb("w_r", [P, KD, E])
        a_neg = sb("a_neg", [P, DB, NS])
        conv_w = sb("conv_w", [P, DB, KC])
        dt_w = sb("dt_w", [P, DB])
        dt_b = sb("dt_b", [P, DB])
        d_skip = sb("d_skip", [P, DB])
        n_w = sb("n_w", [P, KD])
        n_b = sb("n_b", [P, KD])
        neg_half = sb("neg_half", [P, TJ])
        xt = sb("xt", [P, TJ, D])
        st_a = sb("st_a", [P, TJ, 6])
        mv_a = sb("mv_a", [P, TJ, 2])
        ve_a = sb("ve_a", [P, TJ])
        rs_a = sb("rs_a", [P, TJ])
        xn = xt
        xnT = sb("xnT", [P, KD, T])
        hin = sb("hin", [P, DB, T + KC - 1])
        cv = sb("cv", [P, DB, T])
        h = [sb(f"h{i}", [P, DB, T]) for i in range(2)]
        dt = [sb(f"dt{i}", [P, DB, T]) for i in range(2)]
        bcf = sb("bcf", [2 * NS + 1, T])
        hT = [sb(f"hT{i}", [P, TJ, DI]) for i in range(2)]
        pT = [sb(f"pT{i}", [P, TJ, 2 * NS + 1]) for i in range(2)]
        xb = sb("xb", [P, XB, TJ, DI])
        z = cv
        small = sb("small", [P, DB, T], U8)
        da = sb("da", [P, DA, T])
        state = sb("state", [P, 2, DB, T])
        carry = sb("carry", [P, NS, DB])
        prod = sb("prod", [P, 4, T])
        c_row = sb("c_row", [P, 2, 4, T])
        yv = sb("yv", [P, DB, T])
        ez = yv
        xr = sb("xr", [P, TJ, D])
        st_q = sb("st_q", [P, TJ, 6])
        mv_q = sb("mv_q", [P, TJ, 2])
        ve_q = sb("ve_q", [P, TJ])
        rs_q = sb("rs_q", [P, TJ])
        x1 = sb("x1", [P, TJ, D])
        x1T = sb("x1T", [P, KD, T])
        zeros = x1[:, :, :].rearrange("p j d -> p (j d)")
        ser = [xnT[:, 0, :], xnT[:, 1, :], x1T[:, 0, :], x1T[:, 1, :]]
        mx = sb("mx", [P, TJ])
        lg = sb("lg", [P, TJ, E])
        ex = sb("ex", [P, TJ, E])
        su = sb("su", [P, TJ])
        rsu = sb("rsu", [P, TJ])
        pr = sb("pr", [P, TJ, E])
        pr2 = sb("pr2", [P, TJ, E])
        pk = sb("pk", [P, TOPK, TJ])
        eq = sb("eq", [P, TJ, E])
        wr = sb("wr", [P, TJ, E])
        wm = sb("wm", [P, TJ])
        oh = sb("oh", [P, TOPK, TJ, E])
        hot = sb("hot", [P, TJ, E])
        hot_sum = sb("hot_sum", [P, E])
        hot_before = sb("hot_before", [P, E])
        po = sb("po", [P, TOPK * TJ, E])
        bo = sb("bo", [P, TOPK * TJ, E])
        pos_k = sb("pos_k", [P, TOPK * TJ])
        base_k = sb("base_k", [P, TOPK * TJ])
        keep = sb("keep", [P, TOPK * TJ])
        den = sb("den", [P, TJ])
        rden = sb("rden", [P, TJ])
        gk = sb("gk", [P, TOPK, TJ])
        kpos = sb("kpos", [P, TOPK * TJ])
        far = sb("far", [P, TOPK * TJ])
        sidx = sb("sidx", [P, TOPK * TJ], U32)

        y_ps = ps("y_ps", [P, DB, T])
        u_ps = ps("u_ps", [P, 2, T])
        a_ps = ps("a_ps", [P, T])
        q_ps = ps("q_ps", [P, T])

        passed = [sem(f"passed_{n}") for n in ("sp", "pool", "dve", "pe")]
        params = sem("params")
        neg_set = sem("neg_set")
        pool_set = sem("pool_set")
        x_in = sem("x_in")
        xr_in = sem("xr_in")
        c_out = sem("c_out")
        c_in = [sem("c_in0"), sem("c_in1")]
        x1_out = sem("x1_out")
        slotted = sem("slotted")
        a_full = sem("a_full")
        q_full = sem("q_full")
        stat_a = sem("stat_a")
        rstd_a = sem("rstd_a")
        xnT_set = sem("xnT_set")
        hin_set = sem("hin_set")
        conv = sem("conv")
        halo = sem("halo")
        h_set = sem("h_set")
        hT_set = [sem("hT_dve"), sem("hT_act")]
        pT_set = sem("pT_set")
        rows_set = sem("rows_set")
        z_set = sem("z_set")
        soft = sem("soft")
        series = sem("series")
        dt_set = sem("dt_set")
        da_set = sem("da_set")
        xb_act = sem("xb_act")
        xb_dve = sem("xb_dve")
        u_set = sem("u_set")
        scan = sem("scan")
        carried = sem("carried")
        prod_set = sem("prod_set")
        summed = sem("summed")
        y_out = sem("y_out")
        y_silu = sem("y_silu")
        res = sem("res")
        rstd_q = sem("rstd_q")
        x1T_set = sem("x1T_set")
        route = sem("route")
        e_set = sem("e_set")

        block = ctx.enter_context(nc.Block())
        x_dram, expert_in, x1_dram, c_dram = io["x"], scr["expert_in"], scr["x1"], scr["c"]

        def tokens(c):
            return bass.ds(c * T, T)

        @block.sync
        def _(sp):
            for dst, src in ((cst[:, :], io["consts"]), (w_in[:, :, :], io["w_in"].rearrange("(k p) n -> p k n", p=P)),
                             (w_out[:, :, :], io["w_out"].rearrange("(k p) n -> p k n", p=P)),
                             (w_x[:, :, :], io["w_x"].rearrange("(k p) n -> p k n", p=P)),
                             (w_r[:, :, :], io["w_router"].rearrange("(k p) n -> p k n", p=P)),
                             (a_neg[:, :, :], io["a_log"].rearrange("(k p) n -> p k n", p=P)),
                             (conv_w[:, :, :], io["conv_w"].rearrange("(k p) n -> p k n", p=P)),
                             (dt_w[:, :], io["dt_w"]), (dt_b[:, :], io["dt_b"]), (d_skip[:, :], io["d_skip"]),
                             (n_w[:, :], io["n_w"]), (n_b[:, :], io["n_b"])):
                sp.dma_start(dst, src).then_inc(params, 16)
            sp.sem_inc(x1_out, 1)

            def c_rows(c, q):
                wait(sp, prod_set, c * UNITS + 16 * (q - 1))
                sp.dma_start(c_row[:, q % 2, :, :], c_dram[4 * q:4 * q + 4, tokens(c)].partition_broadcast(P)
                             ).then_inc(c_in[q % 2], 16)

            def body(s):
                c = s.c
                if s.a:
                    wait(sp, xnT_set, KD * (c + 1))
                    sp.dma_start(xt[:, :, :], x_dram[tokens(c + 1), :].rearrange("(j p) d -> p j d", p=P)
                                 ).then_inc(x_in, 16)
                if s.q:
                    sp.wait_ge(res, 1 + 5 * (c - 1))
                    sp.dma_start(xr[:, :, :], x_dram[tokens(c - 1), :].rearrange("(j p) d -> p j d", p=P)
                                 ).then_inc(xr_in, 16)
                if s.scan:
                    c_rows(c, 1)
                    c_rows(c, 2)
                if s.q:
                    sp.wait_ge(res, 1 + 5 * c)
                    sp.dma_start(x1_dram[tokens(c - 1), :].rearrange("(j p) d -> p j d", p=P), x1[:, :, :]
                                 ).then_inc(x1_out, 16)
                if s.scan:
                    c_rows(c, 3)
                if s.a:
                    sp.wait_ge(rows_set, c + 2)
                    hold(sp, passed[0])
                    sp.dma_start(c_dram[:, tokens(c + 1)], bcf[NS + 1:2 * NS + 1, :]).then_inc(c_out, 16)
                    sp.wait_ge(c_out, 16 * (c + 2))
                    c_rows(c + 1, 0)

            steps_of(sp.Fori, body)
            sp.wait_ge(x1_out, 1 + 16 * NC)

        @block.gpsimd
        def _(pool):
            pool.memset(neg_half[:, :], -0.5).then_inc(pool_set, 1)
            pool.memset(zeros, 0.0).then_inc(pool_set, 1)
            pool.memset(carry[:, :, :], 0.0).then_inc(pool_set, 1)
            pool.memset(hot_before[:, :], 0.0).then_inc(pool_set, 1)
            pool.memset(hot_sum[:, :], 0.0).then_inc(pool_set, 1)
            pool.memset(hin[:, :, 0:KC - 1], 0.0).then_inc(pool_set, 1)

            pool.wait_ge(pool_set, 2)
            slots = expert_in[0:SLOTS, :].rearrange("(p r) d -> p (r d)", p=P)
            for k in range(ZEROS):
                pool.dma_start(slots[:, k * 1024:(k + 1) * 1024], zeros).then_inc(slotted, 16)

            def unit(s, u):
                n, db = divmod(u, DB)
                g = s.c * UNITS + u
                if u % 16 == 0:
                    q = n // 4
                    pool.wait_ge(c_in[q % 2], 16 * (2 * s.c + q // 2 + 1))
                pool.wait_ge(scan, g + 1)
                wait(pool, summed, g - 3)
                pool.tensor_tensor(prod[:, u % 4, :], state[:, n % 2, db, :], c_row[:, (n // 4) % 2, n % 4, :],
                                   ALU.mult).then_inc(prod_set, 1)

            def rstd(src, ve, rs, done, ready, need, k):
                pool.wait_ge(ready, need)
                hold(pool, passed[1])
                pool.tensor_scalar(ve[:, :], src[:, :, 1], EPS, None, ALU.add).then_inc(done, 1)
                pool.wait_ge(done, 2 * k + 1)
                pool.tensor_tensor(rs[:, :], ve[:, :], neg_half[:, :], ALU.pow).then_inc(done, 1)

            def softplus_series(s, db):
                c = s.c
                pool.wait_ge(soft, 3 * (c + 1) + 2)
                wait(pool, dt_set, 3 * DB * (c + 1))
                hold(pool, passed[1])
                pool.tensor_scalar(ser[db], ez[:, db, :], -0.5, 1.0, ALU.mult, ALU.add).then_inc(series, 1)
                pool.wait_ge(series, 2 * (DB * (c + 1) + db) + 1)
                pool.tensor_tensor(ser[db], ser[db], ez[:, db, :], ALU.mult).then_inc(series, 1)

            def scatter(s, col):
                if col == 0:
                    pool.wait_ge(route, ROUTE * s.c)
                    pool.wait_ge(slotted, 16 * ZEROS)
                    hold(pool, passed[1])
                pool.indirect_dma_start(expert_in[:, :], bass.IndirectOffsetOnAxis(sidx[:, col:col + 1], 0),
                                        x1[:, col % TJ, :], None).then_inc(slotted, 16)

            def body(s):
                for u in range(UNITS if s.scan else 1):
                    if s.scan:
                        unit(s, u)
                    if s.a and (u == 1 or not s.scan):
                        rstd(mv_a, ve_a, rs_a, rstd_a, stat_a, 3 * (s.c + 1) + 2, s.c + 1)
                    if s.q and (u == 27 or not s.scan):
                        rstd(mv_q, ve_q, rs_q, rstd_q, res, 1 + 5 * (s.c - 1) + 4, s.c - 1)
                    for db in range(DB):
                        if s.a and (u == 53 + db or not s.scan):
                            softplus_series(s, db)
                    for col in range(TOPK * TJ):
                        if s.q and (u == 42 + 2 * col - (col > 5) or not s.scan):
                            scatter(s, col)

            steps_of(pool.Fori, body)
            pool.wait_ge(slotted, 16 * (ZEROS + TOPK * TJ * NC))

        @block.scalar
        def _(act):
            act.wait_ge(params, 16 * N_PARAMS)
            act.activation(a_neg[:, :, :], a_neg[:, :, :], ACT.Exp).then_inc(neg_set, 1)
            act.wait_ge(neg_set, 1)
            act.mul(a_neg[:, :, :], a_neg[:, :, :], -1.0).then_inc(neg_set, 1)
            act.wait_ge(neg_set, 2)
            act.sem_inc(y_silu, 1)

            def unit(s, u):
                n, db = divmod(u, DB)
                g = s.c * UNITS + u
                if u < DB:
                    act.wait_ge(dt_set, 3 * (DB * s.c + db + 1))
                wait(act, scan, g - DA + 1)
                act.activation(da[:, u % DA, :], dt[s.par][:, db, :], ACT.Exp, scale=a_neg[:, db, n:n + 1]
                               ).then_inc(da_set, 1)

            def times_b(c, par, n, j):
                if n == 0 and j == 0:
                    act.wait_ge(pT_set, c + 1)
                    act.wait_ge(hT_set[0], 2 * (c + 1))
                    act.wait_ge(hT_set[1], 2 * (c + 1))
                wait(act, u_set, c * UNITS + DB * (n - XB + 1))
                act.mul(xb[:, n % XB, j, :], hT[par][:, j, :], pT[par][:, j, n + 1:n + 2]).then_inc(xb_act, 1)

            def take_hT(s, j):
                act.wait_ge(a_full, s.a_count(f"hT{j}"))
                wait(act, xb_dve, NS * s.c)
                act.copy(hT[1 - s.par][:, j, :], a_ps[:, :]).then_inc(hT_set[1], 1)

            def take_xT(s, k):
                act.wait_ge(a_full, s.a_count(f"xT{k}"))
                act.activation(xnT[:, k, :], a_ps[:, :], ACT.Identity, scale=n_w[:, k:k + 1], bias=n_b[:, k:k + 1]
                               ).then_inc(xnT_set, 1)

            def take_in(s, db):
                if db == 0:
                    wait(act, halo, s.c + 1)
                    act.wait_ge(pool_set, 6)
                act.wait_ge(a_full, s.a_count(f"in{db}"))
                act.copy(hin[:, db, KC - 1:KC - 1 + T], a_ps[:, :]).then_inc(hin_set, 1)

            def silu_h(s):
                c = s.c
                act.wait_ge(conv, KC * DB * (c + 2))
                wait(act, y_out, DB * c)
                act.activation(h[1 - s.par][:, :, :], cv[:, :, :], ACT.Silu).then_inc(h_set, 1)

            def softplus_exp(s):
                c = s.c
                act.wait_ge(z_set, DB * (c + 2))
                wait(act, dt_set, 3 * DB * (c + 1))
                act.activation(ez[:, :, :], z[:, :, :], ACT.Abs).then_inc(soft, 1)
                act.wait_ge(soft, 3 * (c + 1) + 1)
                act.activation(ez[:, :, :], ez[:, :, :], ACT.Exp, scale=-1.0).then_inc(soft, 1)

            def softplus_ln(s):
                act.wait_ge(soft, 3 * (s.c + 1) + 2)
                act.activation(dt[1 - s.par][:, :, :], ez[:, :, :], ACT.Ln, bias=1.0).then_inc(soft, 1)

            def silu_y(s):
                act.wait_ge(y_out, DB * s.c)
                act.activation(yv[:, :, :], yv[:, :, :], ACT.Silu).then_inc(y_silu, 1)

            def take_x1T(s, k):
                act.wait_ge(q_full, s.q_count(f"x1T{k}"))
                act.copy(x1T[:, k, :], q_ps[:, :]).then_inc(x1T_set, 1)

            def exp_logits(s):
                act.wait_ge(route, ROUTE * (s.c - 1) + 2)
                act.activation(ex[:, :, :], lg[:, :, :], ACT.Exp).then_inc(e_set, 1)

            def stages(s, u):
                whole = not s.scan
                for k in range(KD):
                    if s.a and (u == 11 + 3 * k or whole):
                        take_xT(s, k)
                if s.q and (u == 9 or whole):
                    silu_y(s)
                for db in range(DB):
                    if s.a and (u == 17 + 3 * db or whole):
                        take_in(s, db)
                if s.a and (u == 35 or whole):
                    silu_h(s)
                for k in range(KD):
                    if s.q and (u == 34 + 3 * k or whole):
                        take_x1T(s, k)
                for j in (1, 3):
                    if s.a and (u == 39 + 5 * (j // 2) or whole):
                        take_hT(s, j)
                if s.q and (u == 40 or whole):
                    exp_logits(s)
                if s.a and (u == 53 or whole):
                    softplus_exp(s)
                if s.a and (u == 55 or whole):
                    softplus_ln(s)

            def body(s):
                for u in range(UNITS if s.scan else 1):
                    if s.scan:
                        unit(s, u)
                        n, j = divmod(u + 4, TJ)
                        if j < TJ - 1 and n < NS:
                            times_b(s.c, s.par, n, j)
                    stages(s, u)
                    if s.a and s.scan and u >= UNITS - 4 and u % TJ < TJ - 1:
                        times_b(s.c + 1, 1 - s.par, 0, u % TJ)
                if not s.scan and s.a:
                    for j in range(TJ - 1):
                        times_b(0, 0, 0, j)

            steps_of(act.Fori, body)

        @block.vector
        def _(dve):
            dve.wait_ge(params, 16 * N_PARAMS)
            dve.sem_inc(res, 1)
            dve.wait_ge(pool_set, 6)

            def times_b(c, par, n):
                wait(dve, u_set, c * UNITS + DB * (n - XB + 1))
                if n == 0:
                    dve.wait_ge(hT_set[1], 2 * (c + 1))
                    dve.wait_ge(pT_set, c + 1)
                dve.tensor_scalar(xb[:, n % XB, TJ - 1, :], hT[par][:, TJ - 1, :], pT[par][:, TJ - 1, n + 1:n + 2], None,
                                  ALU.mult).then_inc(xb_dve, 1)

            def run_scan(s, u):
                n, db = divmod(u, DB)
                g = s.c * UNITS + u
                dve.wait_ge(u_set, g + 1)
                dve.wait_ge(da_set, g + 1)
                wait(dve, prod_set, g - 7)
                if db == 0:
                    wait(dve, carried, NS * s.c + n - 1)
                dve.tensor_tensor_scan(state[:, n % 2, db, :], da[:, u % DA, :], u_ps[:, u % 2, :],
                                       carry[:, n, db:db + 1], ALU.mult, ALU.add).then_inc(scan, 1)

            def keep_carry(s, n):
                dve.wait_ge(scan, s.c * UNITS + DB * (n + 1))
                dve.tensor_copy(carry[:, n, :], state[:, n % 2, :, T - 1]).then_inc(carried, 1)

            def norm_x(s):
                c = s.c
                dve.wait_ge(x_in, 16 * (c + 2))
                for j in range(TJ):
                    i = dve.bn_stats(st_a[:, j, :], xt[:, j, :])
                i.then_inc(stat_a, 1)
                dve.wait_ge(stat_a, 3 * (c + 1) + 1)
                hold(dve, passed[2])
                for j in range(TJ):
                    i = dve.bn_aggr(mv_a[:, j, :], st_a[:, j, :])
                i.then_inc(stat_a, 1)

            def norm_x_end(s):
                c = s.c
                dve.wait_ge(stat_a, 3 * (c + 1) + 2)
                dve.wait_ge(rstd_a, 2 * (c + 2))
                wait(dve, xnT_set, 2 * (c + 1))
                for j in range(TJ):
                    i = dve.tensor_scalar(xn[:, j, :], xt[:, j, :], mv_a[:, j, 0:1], rs_a[:, j:j + 1],
                                          ALU.subtract, ALU.mult)
                i.then_inc(stat_a, 1)

            def conv_tap(s, db, k):
                c = s.c
                m = KC * DB * (c + 1) + KC * db + k
                w = conv_w[:, db, k:k + 1]
                if k == 0:
                    dve.wait_ge(hin_set, DB * (c + 1) + db + 1)
                    if db == 0:
                        wait(dve, soft, 3 * (c + 1))
                    dve.tensor_scalar(cv[:, db, :], hin[:, db, 0:T], w, None, ALU.mult).then_inc(conv, 1)
                else:
                    dve.wait_ge(conv, m)
                    dve.scalar_tensor_tensor(out=cv[:, db, :], in0=hin[:, db, k:k + T], scalar=w, in1=cv[:, db, :],
                                             op0=ALU.mult, op1=ALU.add).then_inc(conv, 1)

            def move_halo(s):
                dve.wait_ge(conv, KC * DB * (s.c + 2))
                dve.tensor_copy(hin[:, :, 0:KC - 1], hin[:, :, T:T + KC - 1]).then_inc(halo, 1)

            def take_hT(s, j):
                dve.wait_ge(a_full, s.a_count(f"hT{j}"))
                wait(dve, xb_act, (TJ - 1) * NS * s.c)
                dve.tensor_copy(hT[1 - s.par][:, j, :], a_ps[:, :]).then_inc(hT_set[0], 1)

            def take_pT(s):
                dve.wait_ge(a_full, s.a_count("pT"))
                wait(dve, xb_act, (TJ - 1) * NS * s.c)
                dve.tensor_copy(pT[1 - s.par][:, :, :], a_ps[:, 0:TJ * (2 * NS + 1)].rearrange("p (j n) -> p j n", j=TJ)
                                ).then_inc(pT_set, 1)

            def take_rows(s):
                dve.wait_ge(a_full, s.a_count("rows"))
                wait(dve, c_out, 16 * (s.c + 1))
                dve.tensor_copy(bcf[:, :], a_ps[0:2 * NS + 1, :]).then_inc(rows_set, 1)

            def take_dt(s):
                c = s.c
                dve.wait_ge(a_full, s.a_count("dt"))
                dve.wait_ge(h_set, c + 2)
                for db in range(DB):
                    i = dve.tensor_scalar(z[:, db, :], a_ps[:, :], dt_w[:, db:db + 1], dt_b[:, db:db + 1],
                                          ALU.mult, ALU.add).then_inc(z_set, 1)

            def finish_dt(s, db):
                c, d = s.c, dt[1 - s.par]
                k = DB * (c + 1) + db
                dve.wait_ge(soft, 3 * (c + 2))
                dve.tensor_scalar(small[:, db, :], ez[:, db, :], TINY, None, ALU.is_lt).then_inc(dt_set, 1)
                dve.wait_ge(dt_set, 3 * k + 1)
                dve.wait_ge(series, 2 * (k + 1))
                hold(dve, passed[2])
                dve.copy_predicated(d[:, db, :], small[:, db, :], ser[db]).then_inc(dt_set, 1)
                dve.wait_ge(dt_set, 3 * k + 2)
                dve.scalar_tensor_tensor(out=d[:, db, :], in0=z[:, db, :], scalar=0.0, in1=d[:, db, :],
                                         op0=ALU.max, op1=ALU.add).then_inc(dt_set, 1)

            def take_y(s, db):
                dve.wait_ge(summed, s.c * UNITS - DB + db + 1)
                if db == 0:
                    wait(dve, y_silu, s.c)
                dve.scalar_tensor_tensor(out=yv[:, db, :], in0=h[1 - s.par][:, db, :], scalar=d_skip[:, db:db + 1],
                                         in1=y_ps[:, db, :], op0=ALU.mult, op1=ALU.add).then_inc(y_out, 1)

            def residual(s, half):
                k = 1 + 5 * (s.c - 1)
                dve.wait_ge(q_full, s.q_count(f"op{half}"))
                if half == 0:
                    dve.wait_ge(xr_in, 16 * s.c)
                r = xr[:, 2 * half:2 * half + 2, :].rearrange("p a b -> p (a b)")
                dve.scalar_tensor_tensor(out=r, in0=r, scalar=2.0, in1=q_ps[:, :], op0=ALU.mult, op1=ALU.add
                                         ).then_inc(res, 1)
                dve.wait_ge(res, k + half + 1)

            def stats_q(s):
                k = 1 + 5 * (s.c - 1)
                for j in range(TJ):
                    i = dve.bn_stats(st_q[:, j, :], xr[:, j, :])
                i.then_inc(res, 1)
                dve.wait_ge(res, k + 3)
                hold(dve, passed[2])
                for j in range(TJ):
                    i = dve.bn_aggr(mv_q[:, j, :], st_q[:, j, :])
                i.then_inc(res, 1)

            def norm_q(s):
                c = s.c
                dve.wait_ge(res, 1 + 5 * (c - 1) + 4)
                dve.wait_ge(rstd_q, 2 * c)
                dve.wait_ge(x1_out, 1 + 16 * (c - 1))
                dve.wait_ge(slotted, 16 * (ZEROS + TOPK * TJ * (c - 1)))
                for j in range(TJ):
                    i = dve.tensor_scalar(x1[:, j, :], xr[:, j, :], mv_q[:, j, 0:1], rs_q[:, j:j + 1],
                                          ALU.subtract, ALU.mult)
                i.then_inc(res, 1)

            def over_e(a):
                return a.unsqueeze(2).to_broadcast([P, TJ, E])

            def routing(s, part):
                c = s.c
                n = [{0: 0, 1: 2, 2: 20}[part]]
                r0 = ROUTE * (c - 1)

                def done(i):
                    n[0] += 1
                    i.then_inc(route, 1)
                    dve.wait_ge(route, r0 + n[0])

                if part == 0:
                    dve.wait_ge(q_full, s.q_count("rt"))
                    logits = q_ps[:, 0:TJ * E].rearrange("p (j e) -> p j e", e=E)
                    done(dve.tensor_reduce(mx[:, :], logits, AX.X, ALU.max))
                    done(dve.tensor_tensor(lg[:, :, :], logits, over_e(mx[:, :]), ALU.subtract))
                if part == 1:
                    dve.wait_ge(e_set, c)
                    done(dve.tensor_reduce(su[:, :], ex[:, :, :], AX.X, ALU.add))
                    done(dve.reciprocal(rsu[:, :], su[:, :]))
                    done(dve.tensor_tensor(pr[:, :, :], ex[:, :, :], over_e(rsu[:, :]), ALU.mult))
                    src = pr
                    for k in range(TOPK):
                        done(dve.tensor_reduce(pk[:, k, :], src[:, :, :], AX.X, ALU.max))
                        done(dve.tensor_tensor(eq[:, :, :], src[:, :, :], over_e(pk[:, k, :]), ALU.is_equal))
                        done(dve.tensor_tensor(wr[:, :, :], eq[:, :, :], rank, ALU.mult))
                        done(dve.tensor_reduce(wm[:, :], wr[:, :, :], AX.X, ALU.max))
                        done(dve.tensor_tensor(oh[:, k, :, :], wr[:, :, :], over_e(wm[:, :]), ALU.is_equal))
                        if k == 0:
                            done(dve.scalar_tensor_tensor(
                                out=pr2[:, :, :].rearrange("p a b -> p (a b)"),
                                in0=oh[:, 0, :, :].rearrange("p a b -> p (a b)"), scalar=-2.0,
                                in1=pr[:, :, :].rearrange("p a b -> p (a b)"), op0=ALU.mult, op1=ALU.add))
                            src = pr2
                    done(dve.tensor_tensor(hot_before[:, :], hot_before[:, :], hot_sum[:, :], ALU.add))
                    done(dve.tensor_tensor(hot[:, :, :], oh[:, 0, :, :], oh[:, 1, :, :], ALU.add))
                    done(dve.tensor_reduce(hot_sum[:, :], hot[:, :, :].rearrange("p j e -> p e j"), AX.X, ALU.add))
                    done(dve.tensor_tensor(den[:, :], pk[:, 0, :], pk[:, 1, :], ALU.add))
                if part == 2:
                    posn = q_ps[:, 0:TJ * E].rearrange("p (j e) -> p j e", e=E)
                    ohf = oh[:, :, :, :].rearrange("p k j e -> p (k j) e")
                    dve.wait_ge(q_full, s.q_count("pos"))
                    done(dve.tensor_tensor(po[:, 0:TJ, :], oh[:, 0, :, :], posn, ALU.mult))
                    done(dve.tensor_tensor(po[:, TJ:2 * TJ, :], oh[:, 1, :, :], posn, ALU.mult))
                    done(dve.tensor_reduce(pos_k[:, :], po[:, :, :], AX.X, ALU.add))
                    done(dve.tensor_tensor(bo[:, :, :], ohf, base8, ALU.mult))
                    done(dve.tensor_reduce(base_k[:, :], bo[:, :, :], AX.X, ALU.add))
                    done(dve.tensor_scalar(keep[:, :], pos_k[:, :], float(CAP), None, ALU.is_lt))
                    done(dve.reciprocal(rden[:, :], den[:, :]))
                    done(dve.tensor_tensor(gk[:, :, :], pk[:, :, :],
                                           rden[:, :].unsqueeze(1).to_broadcast([P, TOPK, TJ]), ALU.mult))
                    done(dve.tensor_tensor(gates[:, bass.ds((c - 1) * 8, 8)], gk[:, :, :].rearrange("p k j -> p (k j)"),
                                           keep[:, :], ALU.mult))
                    done(dve.tensor_tensor(kpos[:, :], keep[:, :], pos_k[:, :], ALU.mult))
                    done(dve.tensor_tensor(slot_of[:, bass.ds((c - 1) * 8, 8)], kpos[:, :], base_k[:, :], ALU.add))
                    trash = cst[:, bass.ds((c - 1) * 8 + C_TRASH, 8)]
                    done(dve.tensor_tensor(kpos[:, :], kpos[:, :], base_k[:, :], ALU.add))
                    done(dve.tensor_tensor(far[:, :], kpos[:, :], trash, ALU.subtract))
                    done(dve.tensor_tensor(far[:, :], far[:, :], keep[:, :], ALU.mult))
                    done(dve.tensor_tensor(sidx[:, :], far[:, :], trash, ALU.add))
                    assert n[0] == ROUTE

            def stages(s, u):
                whole = not s.scan
                if s.a and (u == 0 or whole):
                    norm_x(s)
                for db in range(DB):
                    if s.q and (u == db or whole):
                        take_y(s, db)
                if s.a and (u == 4 or whole):
                    norm_x_end(s)
                if s.q and (u == 13 or whole):
                    residual(s, 0)
                for db in range(DB):
                    for k in range(KC):
                        if s.a and (u == 14 + 4 * db + k or whole):
                            conv_tap(s, db, k)
                if s.q and (u == 25 or whole):
                    residual(s, 1)
                    stats_q(s)
                if s.q and (u == 29 or whole):
                    norm_q(s)
                if s.a and (u == 30 or whole):
                    move_halo(s)
                if s.a and (u == 34 or whole):
                    take_hT(s, 0)
                if s.q and (u == 35 or whole):
                    routing(s, 0)
                if s.q and (u == 38 or whole):
                    routing(s, 1)
                if s.a and (u == 39 or whole):
                    take_hT(s, 2)
                if s.q and (u == 41 or whole):
                    routing(s, 2)
                if s.a and (u == 44 or whole):
                    take_pT(s)
                if s.a and (u == 46 or whole):
                    take_rows(s)
                if s.a and (u == 48 or whole):
                    take_dt(s)
                for db in range(DB):
                    if s.a and (u == 57 + db or whole):
                        finish_dt(s, db)

            def body(s):
                if not s.scan:
                    stages(s, 0)
                    if s.a:
                        times_b(0, 0, 0)
                    return
                for u in range(UNITS):
                    run_scan(s, u)
                    if u % DB == 1 and u > DB:
                        keep_carry(s, u // DB - 1)
                    if u % DB == 0 and u + DB < UNITS:
                        times_b(s.c, s.par, u // DB + 1)
                    stages(s, u)
                    if u == UNITS - DB and s.a:
                        times_b(s.c + 1, 1 - s.par, 0)
                keep_carry(s, NS - 1)

            steps_of(dve.Fori, body)

        @block.tensor
        def _(pe):
            pe.wait_ge(params, 16 * N_PARAMS)

            def turn_b(c, u):
                n, db = divmod(u, DB)
                if db == 0:
                    pe.wait_ge(xb_act, (TJ - 1) * (NS * c + n + 1))
                    pe.wait_ge(xb_dve, NS * c + n + 1)
                wait(pe, scan, c * UNITS + u - 1)
                for j in range(TJ):
                    i = pe.transpose(u_ps[:, u % 2, j * P:(j + 1) * P], xb[:, n % XB, j, db * P:(db + 1) * P], ident)
                i.then_inc(u_set, 1)

            def add_up(s, u):
                n, db = divmod(u, DB)
                pe.wait_ge(prod_set, s.c * UNITS + u + 1)
                if u < DB:
                    wait(pe, y_out, DB * (s.c - 1) + db + 1)
                pe.matmul(y_ps[:, db, :], ident, prod[:, u % 4, :], start=(n == 0), stop=(n == NS - 1)
                          ).then_inc(summed, 1)

            def take_bank(s, use):
                k = int(use[-1]) if use[-1].isdigit() else 0
                before = {
                    "xT1": (xnT_set, KD * (s.c + 1) + 1), "in0": (xnT_set, KD * (s.c + 2)),
                    "in": (hin_set, DB * (s.c + 1) + k), "hT0": (hin_set, DB * (s.c + 2)),
                    "hT1": (hT_set[0], 2 * (s.c + 1) + 1), "hT2": (hT_set[1], 2 * (s.c + 1) + 1),
                    "hT3": (hT_set[0], 2 * (s.c + 2)), "pT": (hT_set[1], 2 * (s.c + 2)),
                    "rows": (pT_set, s.c + 2), "dt": (rows_set, s.c + 2),
                    "op1": (res, 1 + 5 * (s.c - 1) + 1), "x1T0": (res, 1 + 5 * (s.c - 1) + 2),
                    "x1T1": (x1T_set, KD * (s.c - 1) + 1), "rt": (x1T_set, KD * s.c),
                    "pos": (route, ROUTE * (s.c - 1) + 2),
                }
                key = use if use in before else use[:-1]
                if key in before:
                    pe.wait_ge(*before[key])

            def xT(s, k):
                if k == 0:
                    pe.wait_ge(stat_a, 3 * (s.c + 2))
                take_bank(s, f"xT{k}")
                for j in range(TJ):
                    i = pe.transpose(a_ps[:, j * P:(j + 1) * P], xn[:, j, k * P:(k + 1) * P], ident)
                i.then_inc(a_full, 1)

            def in_proj(s, db, k):
                if k == 0:
                    take_bank(s, f"in{db}")
                i = pe.matmul(a_ps[:, :], w_in[:, k, db * P:(db + 1) * P], xnT[:, k, :],
                              start=(k == 0), stop=(k == KD - 1))
                if k == KD - 1:
                    i.then_inc(a_full, 1)

            def turn_h(s, j):
                if j == 0:
                    pe.wait_ge(h_set, s.c + 2)
                take_bank(s, f"hT{j}")
                for db in range(DB):
                    i = pe.transpose(a_ps[:, db * P:(db + 1) * P], h[1 - s.par][:, db, j * P:(j + 1) * P], ident)
                i.then_inc(a_full, 1)

            def x_proj(s, half):
                if half == 0:
                    take_bank(s, "pT")
                w = 2 * NS + 1
                for j in range(2 * half, 2 * half + 2):
                    for db in range(DB):
                        i = pe.matmul(a_ps[:, j * w:(j + 1) * w], h[1 - s.par][:, db, j * P:(j + 1) * P], w_x[:, db, :],
                                      start=(db == 0), stop=(db == DB - 1))
                if half == 1:
                    i.then_inc(a_full, 1)

            def turn_rows(s):
                take_bank(s, "rows")
                hold(pe, passed[3])
                for j in range(TJ):
                    i = pe.transpose(a_ps[0:2 * NS + 1, j * P:(j + 1) * P], pT[1 - s.par][:, j, :], ident)
                i.then_inc(a_full, 1)

            def spread_dt(s):
                take_bank(s, "dt")
                pe.matmul(a_ps[:, :], ones[0:1, :], bcf[0:1, :], start=True, stop=True).then_inc(a_full, 1)

            def out_proj(s, half, part):
                if half == 0 and part == 0:
                    pe.wait_ge(y_silu, 1 + s.c)
                if part == 0:
                    take_bank(s, f"op{half}")
                jj, pair = divmod(part, 2)
                j = 2 * half + jj
                for db in range(2 * pair, 2 * pair + 2):
                    i = pe.matmul(q_ps[:, jj * D:(jj + 1) * D], yv[:, db, j * P:(j + 1) * P], w_out[:, db, :],
                                  start=(db == 0), stop=(db == DB - 1))
                if part == 3:
                    i.then_inc(q_full, 1)

            def x1_T(s, k):
                if k == 0:
                    pe.wait_ge(res, 1 + 5 * s.c)
                take_bank(s, f"x1T{k}")
                for j in range(TJ):
                    i = pe.transpose(q_ps[:, j * P:(j + 1) * P], x1[:, j, k * P:(k + 1) * P], ident)
                i.then_inc(q_full, 1)

            def router(s):
                pe.wait_ge(x1T_set, 2 * s.c)
                take_bank(s, "rt")
                for j in range(TJ):
                    for k in range(KD):
                        i = pe.matmul(q_ps[:, j * E:(j + 1) * E], x1T[:, k, j * P:(j + 1) * P], w_r[:, k, :],
                                      start=(k == 0), stop=(k == KD - 1))
                i.then_inc(q_full, 1)

            def positions(s):
                pe.wait_ge(route, ROUTE * (s.c - 1) + 20)
                take_bank(s, "pos")
                for j in range(TJ):
                    o = q_ps[:, j * E:(j + 1) * E]
                    pe.matmul(o, tri, hot[:, j, :], start=True, stop=False)
                    for i in range(j):
                        pe.matmul(o, ones, hot[:, i, :], start=False, stop=False)
                    last = pe.matmul(o, ones, hot_before[:, :], start=False, stop=True)
                last.then_inc(q_full, 1)

            def stages(s, u):
                whole = not s.scan
                for k in range(KD):
                    if s.a and (u == 4 + 3 * k or whole):
                        xT(s, k)
                for part in range(4):
                    if s.q and (u == (5, 6, 8, 9)[part] or whole):
                        out_proj(s, 0, part)
                for db in range(DB):
                    for k in range(KD):
                        if s.a and (u == 10 + 3 * db + k or whole):
                            in_proj(s, db, k)
                for part in range(4):
                    if s.q and (u == 12 + 3 * part or whole):
                        out_proj(s, 1, part)
                for k in range(KD):
                    if s.q and (u == 27 + 2 * k or whole):
                        x1_T(s, k)
                for j in range(TJ):
                    if s.a and (u == (30, 32, 35, 37)[j] or whole):
                        turn_h(s, j)
                if s.q and (u == 31 or whole):
                    router(s)
                if s.q and (u == 36 or whole):
                    positions(s)
                for half in range(2):
                    if s.a and (u == 40 + half or whole):
                        x_proj(s, half)
                if s.a and (u == 42 or whole):
                    turn_rows(s)
                if s.a and (u == 44 or whole):
                    spread_dt(s)

            def body(s):
                ahead = 3
                if not s.scan:
                    stages(s, 0)
                    if s.a:
                        for u in range(ahead):
                            turn_b(0, u)
                    return
                for u in range(UNITS):
                    if u + ahead < UNITS:
                        turn_b(s.c, u + ahead)
                    elif s.a:
                        turn_b(s.c + 1, u + ahead - UNITS)
                    add_up(s, u)
                    stages(s, u)

            steps_of(pe.Fori, body)


def experts(nc, io, scr):
    with ExitStack() as ctx:
        def sb(name, shape, dt=F32):
            return ctx.enter_context(nc.sbuf_tensor(name, shape, dt))

        def sem(name):
            return ctx.enter_context(nc.semaphore(name))

        HALF = CAP // 2
        PASSES = ((0, 0), (0, 1), (1, 0))
        XG = KD * CT // 4
        HG = 2 * HB

        ident = sb("ident2", [P, P])
        b1 = sb("b1", [P, HB, E])
        b2 = sb("b2", [P, E, D])
        rows = [sb(f"rows{i}", [P, CT, D]) for i in range(2)]
        xT = [sb(f"xT_{n}", [P, KD * CAP], F32R) for n in ("hi", "lo")]
        w1_raw = sb("w1_raw", [P, KD, H])
        w2_raw = sb("w2_raw", [P, HB, D])
        w1 = [[sb(f"w1_{n}{i}", [P, KD, H], F32R) for n in ("hi", "lo")] for i in range(2)]
        w2 = [[sb(f"w2_{n}{i}", [P, HB, D], F32R) for n in ("hi", "lo")] for i in range(2)]
        b1_e = sb("b1_e", [P, 2, HB])
        relu = sb("relu", [P, 4, HALF])
        hid = [sb(f"hid_{n}", [P, HB, CAP], F32R) for n in ("hi", "lo")]
        eo = sb("eo", [P, CT, D])
        x_ps = ctx.enter_context(nc.psum_tensor("x_ps", [P, 2, 512], F32))
        h_ps = ctx.enter_context(nc.psum_tensor("h_ps", [P, 4, 512], F32))
        o_ps = ctx.enter_context(nc.psum_tensor("o_ps", [P, 2, 512], F32))

        params = sem("params2")
        rows_in = [sem("rows_in0"), sem("rows_in1")]
        w_in = sem("w_in2")
        b1_set = sem("b1_set")
        w_hi = sem("w_hi")
        w_lo = sem("w_lo")
        x_tr = sem("x_tr")
        x_hi = sem("x_hi")
        x_lo = sem("x_lo")
        h_mm = sem("h_mm")
        h_relu = sem("h_relu")
        h_hi = sem("h_hi")
        h_lo = [sem("h_lo_even"), sem("h_lo_odd")]
        o_mm = sem("o_mm")
        o_set = sem("o_set")
        o_out = sem("o_out")

        block = ctx.enter_context(nc.Block())

        def over_experts(engine_loop, body):
            body(0, 0, True)
            with engine_loop(1, E - 2, 2) as e:
                body(e, 1, True)
                body(e + 1, 0, True)
            body(E - 1, 1, False)

        @block.sync
        def _(sp):
            sp.dma_start(ident[:, :], io["consts"][:, C_ID:C_ID + P]).then_inc(params, 16)
            sp.dma_start(b1[:, :, :], io["b1"]).then_inc(params, 16)
            sp.dma_start(b2[:, :, :], io["b2"].partition_broadcast(P)).then_inc(params, 16)

            def load(e, par):
                wait(sp, x_tr, XG * (e - 1))
                sp.dma_start(rows[par][:, :, :], scr["expert_in"][bass.ds(e * CAP, CAP), :]
                             .rearrange("(j p) d -> p j d", p=P)).then_inc(rows_in[par], 16)
                wait(sp, w_lo, 2 * e)
                sp.dma_start(w1_raw[:, :, :], io["w1"][bass.ds(e * D, D), :].rearrange("(k p) n -> p k n", p=P)
                             ).then_inc(w_in, 16)
                sp.dma_start(w2_raw[:, :, :], io["w2"][bass.ds(e * H, H), :].rearrange("(k p) n -> p k n", p=P)
                             ).then_inc(w_in, 16)

            def body(e, par, more):
                if more:
                    load(e + 1, 1 - par)
                for half in range(2):
                    sp.wait_ge(o_set, CT * e + 3 * (half + 1))
                    sp.dma_start(scr["expert_out"][bass.ds(e * CAP + half * HALF, HALF), :]
                                 .rearrange("(j p) d -> p j d", p=P), eo[:, 3 * half:3 * half + 3, :]
                                 ).then_inc(o_out, 16)

            load(0, 0)
            over_experts(sp.Fori, body)
            sp.wait_ge(o_out, 32 * E)

        @block.gpsimd
        def _(pool):
            def split_weights(e, par):
                for k, (w, raw) in enumerate(((w1, w1_raw), (w2, w2_raw))):
                    pool.wait_ge(w_hi, 2 * e + k + 1)
                    pool.tensor_tensor(w[par][1][:, :, :], raw[:, :, :], w[par][0][:, :, :].bitcast(F32), ALU.subtract
                                       ).then_inc(w_lo, 1)

            def body(e, par, more):
                for hb in range(HB):
                    pool.wait_ge(h_hi, HG * e + 2 * hb + 1)
                    pool.tensor_tensor(hid[1][:, hb, 0:HALF], relu[:, 2 * hb % 4, :],
                                       hid[0][:, hb, 0:HALF].bitcast(F32), ALU.subtract).then_inc(h_lo[0], 1)
                if more:
                    split_weights(e + 1, 1 - par)

            split_weights(0, 0)
            over_experts(pool.Fori, body)

        @block.scalar
        def _(act):
            act.wait_ge(params, 48)

            def high_weights(e, par, k):
                if k == 0:
                    act.wait_ge(w_in, 32 * (e + 1))
                    wait(act, o_mm, CT * (e - 1))
                w, raw = ((w1, w1_raw), (w2, w2_raw))[k]
                act.copy(w[par][0][:, :, :], raw[:, :, :]).then_inc(w_hi, 1)

            def high_x(e, par):
                wait(act, h_mm, HG * e)
                for g in range(XG):
                    act.wait_ge(x_tr, XG * e + g + 1)
                    act.copy(xT[0][:, g * 512:(g + 1) * 512], x_ps[:, (par + g) % 2, :]).then_inc(x_hi, 1)

            def body(e, par, more):
                act.copy(b1_e[:, par, :], b1[:, :, bass.ds(e, 1)].rearrange("p h o -> p (h o)")).then_inc(b1_set, 1)
                act.wait_ge(b1_set, e + 1)
                for g in range(HG):
                    hb, half = divmod(g, 2)
                    act.wait_ge(h_mm, HG * e + g + 1)
                    wait(act, h_lo[half], HB * e + hb - 1)
                    act.activation(relu[:, g % 4, :], h_ps[:, g % 4, 0:HALF], ACT.Relu, bias=b1_e[:, par, hb:hb + 1]
                                   ).then_inc(h_relu, 1)
                    if more and g in (3, 9):
                        high_weights(e + 1, 1 - par, g // 9)
                if more:
                    high_x(e + 1, 1 - par)

            high_weights(0, 0, 0)
            high_weights(0, 0, 1)
            high_x(0, 0)
            over_experts(act.Fori, body)

        @block.vector
        def _(dve):
            dve.wait_ge(params, 48)

            def low_x(e, par):
                wait(dve, h_mm, HG * e)
                for g in range(XG):
                    cols = slice(g * 512, (g + 1) * 512)
                    dve.wait_ge(x_hi, XG * e + g + 1)
                    dve.tensor_tensor(xT[1][:, cols], x_ps[:, (par + g) % 2, :], xT[0][:, cols].bitcast(F32),
                                      ALU.subtract).then_inc(x_lo, 1)

            def body(e, par, more):
                wait(dve, o_mm, CT * e)
                for g in range(HG):
                    hb, half = divmod(g, 2)
                    cols = slice(half * HALF, (half + 1) * HALF)
                    dve.wait_ge(h_relu, HG * e + g + 1)
                    dve.tensor_copy(hid[0][:, hb, cols], relu[:, g % 4, :]).then_inc(h_hi, 1)
                    if half == 1:
                        dve.wait_ge(h_hi, HG * e + g + 1)
                        dve.tensor_tensor(hid[1][:, hb, cols], relu[:, g % 4, :], hid[0][:, hb, cols].bitcast(F32),
                                          ALU.subtract).then_inc(h_lo[1], 1)
                if more:
                    low_x(e + 1, 1 - par)
                for j in range(CT):
                    dve.wait_ge(o_mm, CT * e + j + 1)
                    if j % 3 == 0:
                        wait(dve, o_out, 32 * e)
                    dve.tensor_tensor(eo[:, j, :], o_ps[:, j % 2, 0:D],
                                      b2[:, bass.ds(e, 1), :].rearrange("p o d -> p (o d)"), ALU.add).then_inc(o_set, 1)

            low_x(0, 0)
            over_experts(dve.Fori, body)

        @block.tensor
        def _(pe):
            pe.wait_ge(params, 48)

            def turn(e, par):
                pe.wait_ge(rows_in[par], 8 * (e - par) + 16)
                for g in range(XG):
                    wait(pe, x_lo, XG * e + g - 1)
                    for i in range(4):
                        k, j = divmod(4 * g + i, CT)
                        last = pe.transpose(x_ps[:, (par + g) % 2, i * P:(i + 1) * P], rows[par][:, j, k * P:(k + 1) * P],
                                            ident[:, :])
                    last.then_inc(x_tr, 1)

            def hidden(e, par):
                pe.wait_ge(x_lo, XG * (e + 1))
                pe.wait_ge(w_lo, 2 * e + 1)
                for g in range(HG):
                    hb, half = divmod(g, 2)
                    wait(pe, h_relu, HG * e + g - 3)
                    n = 0
                    for a, b in PASSES:
                        for k in range(KD):
                            c0 = k * CAP + half * HALF
                            last = pe.matmul(h_ps[:, g % 4, 0:HALF], w1[par][a][:, k, hb * P:(hb + 1) * P],
                                             xT[b][:, c0:c0 + HALF], start=(n == 0), stop=(n == 3 * KD - 1))
                            n += 1
                    last.then_inc(h_mm, 1)

            def outputs(e, par):
                pe.wait_ge(h_lo[0], HB * (e + 1))
                pe.wait_ge(h_lo[1], HB * (e + 1))
                pe.wait_ge(w_lo, 2 * e + 2)
                for j in range(CT):
                    wait(pe, o_set, CT * e + j - 1)
                    n = 0
                    for a, b in PASSES:
                        for hb in range(HB):
                            last = pe.matmul(o_ps[:, j % 2, 0:D], hid[a][:, hb, j * P:(j + 1) * P], w2[par][b][:, hb, :],
                                             start=(n == 0), stop=(n == 3 * HB - 1))
                            n += 1
                    last.then_inc(o_mm, 1)

            def body(e, par, more):
                hidden(e, par)
                if more:
                    turn(e + 1, 1 - par)
                outputs(e, par)

            turn(0, 0)
            over_experts(pe.Fori, body)


def combine(nc, scr, gates, slot_of, out):
    with ExitStack() as ctx:
        def sb(name, shape, dt=F32):
            return ctx.enter_context(nc.sbuf_tensor(name, shape, dt))

        def sem(name):
            return ctx.enter_context(nc.semaphore(name))

        got = sb("got", [P, NC, TOPK, TJ, D])
        x1 = sb("x1_all", [P, NC, TJ, D])
        st = sb("st_f", [P, NC, TJ, 6])
        mv = sb("mv_f", [P, NC, TJ, 2])
        ve = sb("ve_f", [P, NC, TJ])
        sd = sb("sd_f", [P, NC, TJ])
        rs = sb("rs_f", [P, NC, TJ])

        rows_in = [sem(f"got{c}") for c in range(NC)]
        x1_in = [sem(f"x1_in{c}") for c in range(NC)]
        mixed = sem("mixed")
        rooted = sem("rooted")
        normed = sem("normed")
        stored = sem("stored")

        block = ctx.enter_context(nc.Block())

        @block.gpsimd
        def _(pool):
            for c in range(NC):
                for k in range(TOPK):
                    for j in range(TJ):
                        col = (c * TOPK + k) * TJ + j
                        pool.indirect_dma_start(got[:, c, k, j, :], None, scr["expert_out"],
                                                bass.IndirectOffsetOnAxis(slot_of[:, col:col + 1], 0)
                                                ).then_inc(rows_in[c], 16)

        @block.sync
        def _(sp):
            for c in range(NC):
                sp.dma_start(x1[:, c, :, :], scr["x1"][c * T:(c + 1) * T, :].rearrange("(j p) d -> p j d", p=P)
                             ).then_inc(x1_in[c], 16)
            with sp.Fori(0, NC) as c:
                sp.wait_ge(normed, 2 * c + 2)
                sp.dma_start(out[bass.ds(c * T, T), :].rearrange("(j p) d -> p j d", p=P),
                             x1[:, bass.ds(c, 1), :, :].rearrange("p o j d -> p (o j) d")).then_inc(stored, 16)
            sp.wait_ge(stored, 16 * NC)

        @block.scalar
        def _(act):
            with act.Fori(0, NC) as c:
                act.wait_ge(mixed, 5 * c + 5)
                act.activation(sd[:, bass.ds(c, 1), :], ve[:, bass.ds(c, 1), :], ACT.Sqrt).then_inc(rooted, 1)

        @block.vector
        def _(dve):
            def mix(c):
                dve.wait_ge(rows_in[c], 16 * TOPK * TJ)
                dve.wait_ge(x1_in[c], 16)
                for k in range(TOPK):
                    for j in range(TJ):
                        col = (c * TOPK + k) * TJ + j
                        i = dve.scalar_tensor_tensor(out=x1[:, c, j, :], in0=got[:, c, k, j, :],
                                                     scalar=gates[:, col:col + 1], in1=x1[:, c, j, :],
                                                     op0=ALU.mult, op1=ALU.add)
                    i.then_inc(mixed, 1)
                    dve.wait_ge(mixed, 5 * c + k + 1)
                for j in range(TJ):
                    i = dve.bn_stats(st[:, c, j, :], x1[:, c, j, :])
                i.then_inc(mixed, 1)
                dve.wait_ge(mixed, 5 * c + 3)
                for j in range(TJ):
                    i = dve.bn_aggr(mv[:, c, j, :], st[:, c, j, :])
                i.then_inc(mixed, 1)
                dve.wait_ge(mixed, 5 * c + 4)
                dve.tensor_scalar(ve[:, c, :], mv[:, c, :, 1], EPS, None, ALU.add).then_inc(mixed, 1)

            def norm(c):
                dve.wait_ge(rooted, c + 1)
                dve.reciprocal(rs[:, c, :], sd[:, c, :]).then_inc(normed, 1)
                dve.wait_ge(normed, 2 * c + 1)
                for j in range(TJ):
                    i = dve.tensor_scalar(x1[:, c, j, :], x1[:, c, j, :], mv[:, c, j, 0:1], rs[:, c, j:j + 1],
                                          ALU.subtract, ALU.mult)
                i.then_inc(normed, 1)

            for c in range(NC):
                mix(c)
                if c > 0:
                    norm(c - 1)
            norm(NC - 1)


def program(nc, io, out):
    scr = {
        "expert_in": nc.dram_tensor("expert_in", (SLOTS + TOPK * L, D), F32, kind="Internal").ap(),
        "expert_out": nc.dram_tensor("expert_out", (SLOTS, D), F32, kind="Internal").ap(),
        "x1": nc.dram_tensor("x1_scratch", (L, D), F32, kind="Internal").ap(),
        "c": nc.dram_tensor("c_scratch", (NS, L), F32, kind="Internal").ap(),
    }
    cols = TOPK * L // P
    with nc.sbuf_tensor("gates", [P, cols], F32) as gates, nc.sbuf_tensor("slot_of", [P, cols], U32) as slot_of:
        mixer_and_routing(nc, io, scr, gates, slot_of)
        experts(nc, io, scr)
        combine(nc, scr, gates, slot_of, out)


def constants():
    import numpy as np

    c = np.zeros((P, C_END), np.float32)
    c[:, C_ID:C_ID + P] = np.eye(P)
    c[:, C_TRI:C_TRI + P] = np.triu(np.ones((P, P)), 1)
    c[:, C_ONE:C_ONE + P] = 1
    c[:, C_RANK:C_RANK + TJ * E] = np.tile(E - np.arange(E), TJ)
    c[:, C_BASE:C_BASE + TOPK * TJ * E] = np.tile(CAP * np.arange(E), TOPK * TJ)
    for ch in range(NC):
        for k in range(TOPK):
            for j in range(TJ):
                t = ch * T + j * P + np.arange(P)
                c[:, C_TRASH + (ch * TOPK + k) * TJ + j] = SLOTS + TOPK * t + k
    return c


def kernel(**inputs):
    import numpy as np
    import concourse.bacc as bacc
    from concourse.bass_utils import run_bass_kernel_spmd

    a = {k.split("_", 2)[2]: np.asarray(v) for k, v in inputs.items() if k.startswith("L0_attn_")}
    f = {k.split("_", 2)[2]: np.asarray(v) for k, v in inputs.items() if k.startswith("L0_ffn_")}
    by_block = lambda v: np.ascontiguousarray(v.reshape(-1, P).T)
    arrays = {
        "x": a["x"].reshape(L, D), "w_in": a["in_proj_w"].T, "w_out": a["out_proj_w"].T, "w_x": a["x_proj_w"].T,
        "w_router": f["w_router"], "a_log": a["A_log"], "conv_w": a["conv_w"], "dt_w": by_block(a["dt_proj_w"]),
        "dt_b": by_block(a["dt_proj_b"]), "d_skip": by_block(a["D"]), "n_w": by_block(a["norm_w"]),
        "n_b": by_block(a["norm_b"]), "w1": f["w1"].reshape(E * D, H), "w2": f["w2"].reshape(E * H, D),
        "b1": f["b1"].reshape(E, HB, P).transpose(2, 1, 0), "b2": f["b2"], "consts": constants(),
    }
    nc = bacc.Bacc("TRN2", target_bir_lowering=False, num_devices=1)
    arrays = {f"in_{k}": np.ascontiguousarray(v) for k, v in arrays.items()}
    io = {k[3:]: nc.dram_tensor(k, v.shape, mybir.dt.from_np(v.dtype), kind="ExternalInput").ap()
          for k, v in arrays.items()}
    out = nc.dram_tensor("out", (L, D), F32, kind="ExternalOutput").ap()
    program(nc, io, out)
    r = run_bass_kernel_spmd(nc, [arrays], core_ids=[0])
    return r.results[0]["out"].reshape(1, L, D)
```

```python
from contextlib import ExitStack

import concourse.bass as bass
from concourse import mybir

F32 = mybir.dt.float32
F32R = mybir.dt.float32r
U32 = mybir.dt.uint32
U8 = mybir.dt.uint8
ALU = mybir.AluOpType
ACT = mybir.ActivationFunctionType
AX = mybir.AxisListType

P = 128
L = 4096
D = 256
DI = 512
NS = 16
KC = 4
T = 512
NC = L // T
TJ = T // P
DB = DI // P
KD = D // P
SP = 2
GC = P // SP
NG = DI // GC
NM = NS // SP
UNITS = NM * NG
DA = 8
XB = 2
PR = 8
CM = 2
E = 8
H = 1024
HB = H // P
TOPK = 2
CAP = int(1.5 * 4 * 512 * TOPK / E)
CT = CAP // P
SLOTS = E * CAP
DX = D + 2
EPS = 1e-5
ROUTE = 36
ZEROS = SLOTS * DX // (P * TJ * DX)
BLANKS = TOPK * L // (P * TJ)
N_PARAMS = 12
TINY = 2.0 ** -8

C_ID, C_TRI, C_ONE, C_RANK, C_BASE, C_TRASH, C_PAIR, C_SPARE, C_END = 0, 128, 256, 384, 416, 480, 544, 608, 614

A_USES = ["xT0", "xT1", "in0", "in1", "in2", "in3", "rows", "dt", "pT", "hT0", "hT1", "hT2", "hT3"]
Q_USES = ["op0", "op1", "x1T0", "x1T1", "rt", "pos"]


class Step:

    def __init__(self, c, par, a=True, scan=True, q=True):
        self.c, self.par, self.a, self.scan, self.q = c, par, a, scan, q

    def a_count(self, use):
        return len(A_USES) * (self.c + 1) + A_USES.index(use) + 1

    def q_count(self, use):
        return len(Q_USES) * (self.c - 1) + Q_USES.index(use) + 1


def steps_of(engine_loop, body):
    body(Step(-1, 1, scan=False, q=False))
    body(Step(0, 0, q=False))
    with engine_loop(1, NC - 2, 2) as c:
        body(Step(c, 1))
        body(Step(c + 1, 0))
    body(Step(NC - 1, (NC - 1) % 2, a=False))
    body(Step(NC, NC % 2, a=False, scan=False))


def wait(eng, sem, value):
    if not isinstance(value, int) or value > 0:
        eng.wait_ge(sem, value)


def hold(eng, passed):
    eng.sem_inc(passed, 1)


def mixer_and_routing(nc, io, scr, gates):
    with ExitStack() as ctx:
        def sb(name, shape, dt=F32):
            return ctx.enter_context(nc.sbuf_tensor(name, shape, dt))

        def ps(name, shape):
            return ctx.enter_context(nc.psum_tensor(name, shape, F32))

        def sem(name):
            return ctx.enter_context(nc.semaphore(name))

        cst = sb("cst", [P, C_END])
        ident, tri, ones = cst[:, C_ID:C_ID + P], cst[:, C_TRI:C_TRI + P], cst[:, C_ONE:C_ONE + P]
        both = cst[:, C_PAIR:C_PAIR + GC]
        rank = cst[:, C_RANK:C_RANK + 32].rearrange("p (j e) -> p j e", e=E)
        base8 = cst[:, C_BASE:C_BASE + 64].rearrange("p (k e) -> p k e", e=E)
        w_in = sb("w_in", [P, KD, DI])
        w_out = sb("w_out", [P, DB, D])
        w_x = sb("w_x", [P, DB, 2 * NS + 1])
        w_r = sb("w_r", [P, KD, E])
        a_neg = sb("a_neg", [P, NG, NM])
        conv_w = sb("conv_w", [P, DB, KC])
        dt_w = sb("dt_w", [P, DB])
        dt_b = sb("dt_b", [P, DB])
        d_skip = sb("d_skip", [P, DB])
        n_w = sb("n_w", [P, KD])
        n_b = sb("n_b", [P, KD])
        neg_half = sb("neg_half", [P, TJ])
        xt = sb("xt", [P, TJ, D])
        st_a = sb("st_a", [P, TJ, 6])
        mv_a = sb("mv_a", [P, TJ, 2])
        ve_a = sb("ve_a", [P, TJ])
        rs_a = sb("rs_a", [P, TJ])
        xn = xt
        xnT = sb("xnT", [P, KD, T])
        hin = sb("hin", [P, DB, T + KC - 1])
        h = [sb(f"h{i}", [P, DB, T]) for i in range(2)]
        dt = sb("dt", [P, DB, T])
        bcf = sb("bcf", [2 * NS + 1, T])
        hT = [sb(f"hT{i}", [P, TJ, DI]) for i in range(2)]
        pT = [sb(f"pT{i}", [P, TJ, 2 * NS + 1]) for i in range(2)]
        xb = sb("xb", [P, XB, TJ, NG, SP, GC])
        z = hin[:, :, KC - 1:]
        small = sb("small", [P, DB, T], U8)
        dt2 = sb("dt2", [P, NG, T])
        da = sb("da", [P, DA, T])
        state = sb("state", [P, 2, DB, T])
        carry = sb("carry", [P, UNITS])
        prod = sb("prod", [P, PR, T])
        c_row = sb("c_row", [P, 2, CM, T])
        yv = sb("yv", [P, DB, T])
        ez = yv
        xr = sb("xr", [P, TJ, D])
        st_q = sb("st_q", [P, TJ, 6])
        mv_q = sb("mv_q", [P, TJ, 2])
        ve_q = sb("ve_q", [P, TJ])
        rs_q = sb("rs_q", [P, TJ])
        x1 = sb("x1", [P, TJ, DX])
        x1T = sb("x1T", [P, KD, T])
        zeros = x1[:, :, :].rearrange("p j d -> p (j d)")
        ser = [xnT, x1T]
        mx = sb("mx", [P, TJ])
        lg = sb("lg", [P, TJ, E])
        ex = sb("ex", [P, TJ, E])
        su = sb("su", [P, TJ])
        rsu = sb("rsu", [P, TJ])
        pr = sb("pr", [P, TJ, E])
        pr2 = sb("pr2", [P, TJ, E])
        pk = sb("pk", [P, TOPK, TJ])
        eq = sb("eq", [P, TJ, E])
        wr = sb("wr", [P, TJ, E])
        wm = sb("wm", [P, TJ])
        oh = sb("oh", [P, TOPK, TJ, E])
        hot = sb("hot", [P, TJ, E])
        hot_sum = sb("hot_sum", [P, E])
        hot_before = sb("hot_before", [P, E])
        po = sb("po", [P, TOPK * TJ, E])
        bo = sb("bo", [P, TOPK * TJ, E])
        pos_k = sb("pos_k", [P, TOPK * TJ])
        base_k = sb("base_k", [P, TOPK * TJ])
        keep = sb("keep", [P, TOPK * TJ])
        den = sb("den", [P, TJ])
        rden = sb("rden", [P, TJ])
        gk = sb("gk", [P, TOPK, TJ])
        kpos = sb("kpos", [P, TOPK * TJ])
        far = sb("far", [P, TOPK * TJ])
        sidx = sb("sidx", [P, TOPK * TJ], U32)

        y_ps = ps("y_ps", [P, DB, T])
        u_ps = ps("u_ps", [P, 2, T])
        a_ps = ps("a_ps", [P, T])
        q_ps = ps("q_ps", [P, T])

        passed = [sem(f"passed_{n}") for n in ("sp", "pool", "dve", "pe")]
        params = sem("params")
        neg_set = sem("neg_set")
        pool_set = sem("pool_set")
        x_in = sem("x_in")
        xr_in = sem("xr_in")
        c_out = sem("c_out")
        c_in = [sem("c_in0"), sem("c_in1")]
        dt2_in = [sem(f"dt2_in{i}") for i in range(DB)]
        x1_out = sem("x1_out")
        blanked = sem("blanked")
        slotted = sem("slotted")
        a_full = sem("a_full")
        q_full = sem("q_full")
        stat_a = sem("stat_a")
        rstd_a = sem("rstd_a")
        xnT_set = sem("xnT_set")
        hin_set = sem("hin_set")
        conv = sem("conv")
        halo = sem("halo")
        h_set = sem("h_set")
        hT_set = [sem("hT_dve"), sem("hT_act")]
        pT_set = sem("pT_set")
        rows_set = sem("rows_set")
        z_set = sem("z_set")
        soft = sem("soft")
        series = sem("series")
        dt_set = sem("dt_set")
        da_set = sem("da_set")
        xb_act = sem("xb_act")
        xb_dve = sem("xb_dve")
        u_set = sem("u_set")
        scan = sem("scan")
        carried = sem("carried")
        prod_set = sem("prod_set")
        summed = sem("summed")
        y_out = sem("y_out")
        y_silu = sem("y_silu")
        res = sem("res")
        rstd_q = sem("rstd_q")
        x1T_set = sem("x1T_set")
        route = sem("route")
        e_set = sem("e_set")

        block = ctx.enter_context(nc.Block())
        x_dram, expert_in, x1_dram = io["x"], scr["expert_in"], scr["x1"]
        c_dram = scr["c"].rearrange("(m s) t -> s m t", s=SP)

        def by_group(channels):
            return channels.rearrange("p (g c) -> p g c", c=GC)

        def tokens(c):
            return bass.ds(c * T, T)

        @block.sync
        def _(sp):
            for dst, src in ((cst[:, :], io["consts"]), (w_in[:, :, :], io["w_in"].rearrange("(k p) n -> p k n", p=P)),
                             (w_out[:, :, :], io["w_out"].rearrange("(k p) n -> p k n", p=P)),
                             (w_x[:, :, :], io["w_x"].rearrange("(k p) n -> p k n", p=P)),
                             (w_r[:, :, :], io["w_router"].rearrange("(k p) n -> p k n", p=P)),
                             (a_neg[:, :, :], io["a_log"]),
                             (conv_w[:, :, :], io["conv_w"].rearrange("(k p) n -> p k n", p=P)),
                             (dt_w[:, :], io["dt_w"]), (dt_b[:, :], io["dt_b"]), (d_skip[:, :], io["d_skip"]),
                             (n_w[:, :], io["n_w"]), (n_b[:, :], io["n_b"])):
                sp.dma_start(dst, src).then_inc(params, 16)
            sp.sem_inc(x1_out, 1)

            def c_rows(c, q):
                wait(sp, prod_set, c * UNITS + (q - 1) * CM * NG)
                hold(sp, passed[0])
                for k in range(SP):
                    sp.dma_start(c_row[k * GC:(k + 1) * GC, q % 2, :, :],
                                 c_dram[k, CM * q:CM * (q + 1), tokens(c)].partition_broadcast(GC)
                                 ).then_inc(c_in[q % 2], 16)

            def spread_dt(c, db):
                sp.wait_ge(dt_set, 3 * (DB * c + db + 1))
                hold(sp, passed[0])
                wait(sp, da_set, (c - 1) * UNITS + UNITS - NG + 2 * db + 2)
                hold(sp, passed[0])
                for half in range(2):
                    for k in range(SP):
                        sp.dma_start(dt2[k * GC:(k + 1) * GC, 2 * db + half, :],
                                     dt[half * GC:(half + 1) * GC, db, :]).then_inc(dt2_in[db], 16)

            def body(s):
                c = s.c
                if s.a:
                    wait(sp, xnT_set, KD * (c + 1))
                    sp.dma_start(xt[:, :, :], x_dram[tokens(c + 1), :].rearrange("(j p) d -> p j d", p=P)
                                 ).then_inc(x_in, 16)
                if s.scan:
                    c_rows(c, 1)
                if s.q:
                    sp.wait_ge(res, 1 + 5 * (c - 1))
                    sp.dma_start(xr[:, :, :], x_dram[tokens(c - 1), :].rearrange("(j p) d -> p j d", p=P)
                                 ).then_inc(xr_in, 16)
                if s.scan:
                    c_rows(c, 2)
                if s.q:
                    sp.wait_ge(res, 1 + 5 * c)
                    sp.dma_start(x1_dram[tokens(c - 1), :].rearrange("(j p) d -> p j d", p=P), x1[:, :, 0:D]
                                 ).then_inc(x1_out, 16)
                if s.scan:
                    c_rows(c, 3)
                if s.scan and not s.q:
                    sp.wait_ge(pool_set, 2)
                    for k in range(BLANKS):
                        sp.dma_start(scr["choice_out"][k * P * TJ:(k + 1) * P * TJ, :]
                                     .rearrange("(p r) d -> p r d", p=P), x1[:, :, 0:D]).then_inc(blanked, 16)
                if s.a:
                    sp.wait_ge(rows_set, c + 2)
                    hold(sp, passed[0])
                    sp.dma_start(scr["c"][:, tokens(c + 1)],
                                 bcf[NS + 1:2 * NS + 1, :]).then_inc(c_out, 16)
                    sp.wait_ge(c_out, 16 * (c + 2))
                    c_rows(c + 1, 0)
                    for db in range(DB):
                        spread_dt(c + 1, db)

            steps_of(sp.Fori, body)
            sp.wait_ge(x1_out, 1 + 16 * NC)

        @block.gpsimd
        def _(pool):
            pool.memset(neg_half[:, :], -0.5).then_inc(pool_set, 1)
            pool.memset(zeros, 0.0).then_inc(pool_set, 1)
            pool.memset(carry[:, :], 0.0).then_inc(pool_set, 1)
            pool.memset(hot_before[:, :], 0.0).then_inc(pool_set, 1)
            pool.memset(hot_sum[:, :], 0.0).then_inc(pool_set, 1)
            pool.memset(hin[:, :, 0:KC - 1], 0.0).then_inc(pool_set, 1)

            def clear_slots():
                pool.wait_ge(pool_set, 2)
                slots = expert_in[0:SLOTS, :].rearrange("(p r) d -> p (r d)", p=P)
                for k in range(ZEROS):
                    pool.dma_start(slots[:, k * TJ * DX:(k + 1) * TJ * DX], zeros).then_inc(slotted, 16)

            def unit(s, u):
                m = u // NG
                t = s.c * UNITS + u
                q = m // CM
                if u % (CM * NG) == 0:
                    pool.wait_ge(c_in[q % 2], 32 * (2 * s.c + q // 2 + 1))
                pool.wait_ge(scan, t + 1)
                wait(pool, summed, t - PR + 1)
                pool.tensor_tensor(prod[:, u % PR, :], state[:, (u // 4) % 2, u % 4, :], c_row[:, q % 2, m % CM, :],
                                   ALU.mult).then_inc(prod_set, 1)

            def rstd(src, ve, rs, done, ready, need, k):
                pool.wait_ge(ready, need)
                hold(pool, passed[1])
                pool.tensor_scalar(ve[:, :], src[:, :, 1], EPS, None, ALU.add).then_inc(done, 1)
                pool.wait_ge(done, 2 * k + 1)
                pool.tensor_tensor(rs[:, :], ve[:, :], neg_half[:, :], ALU.pow).then_inc(done, 1)

            def softplus_series(s, i):
                c = s.c
                pool.wait_ge(soft, 3 * (c + 1) + 2)
                wait(pool, dt_set, 3 * DB * (c + 1))
                hold(pool, passed[1])
                e = ez[:, 2 * i:2 * i + 2, :]
                pool.tensor_scalar(ser[i][:, :, :], e, -0.5, 1.0, ALU.mult, ALU.add).then_inc(series, 1)
                pool.wait_ge(series, 2 * (2 * (c + 1) + i) + 1)
                pool.tensor_tensor(ser[i][:, :, :], ser[i][:, :, :], e, ALU.mult).then_inc(series, 1)

            def scatter(s, col):
                if col == 0:
                    pool.wait_ge(route, ROUTE * s.c)
                    pool.wait_ge(slotted, 16 * ZEROS)
                    hold(pool, passed[1])
                pool.indirect_dma_start(expert_in[:, :], bass.IndirectOffsetOnAxis(sidx[:, col:col + 1], 0),
                                        x1[:, col % TJ, :], None).then_inc(slotted, 16)

            def body(s):
                for u in range(UNITS if s.scan else 1):
                    if s.scan:
                        unit(s, u)
                    if s.a and (u == 2 or not s.scan):
                        rstd(mv_a, ve_a, rs_a, rstd_a, stat_a, 3 * (s.c + 1) + 2, s.c + 1)
                    if s.q and (u == 25 or not s.scan):
                        rstd(mv_q, ve_q, rs_q, rstd_q, res, 1 + 5 * (s.c - 1) + 4, s.c - 1)
                    if s.a and not s.scan:
                        clear_slots()
                    for i in range(2):
                        if s.a and (u == 42 + 2 * i or not s.scan):
                            softplus_series(s, i)
                    for col in range(TOPK * TJ):
                        if s.q and (u == (46, 48, 50, 52, 54, 56, 57, 59)[col] or not s.scan):
                            scatter(s, col)

            steps_of(pool.Fori, body)
            pool.wait_ge(slotted, 16 * (ZEROS + TOPK * TJ * NC))

        @block.scalar
        def _(act):
            act.wait_ge(params, 16 * N_PARAMS)
            act.activation(a_neg[:, :, :], a_neg[:, :, :], ACT.Exp).then_inc(neg_set, 1)
            act.wait_ge(neg_set, 1)
            act.mul(a_neg[:, :, :], a_neg[:, :, :], -1.0).then_inc(neg_set, 1)
            act.wait_ge(neg_set, 2)
            act.sem_inc(y_silu, 1)

            def unit(s, u):
                m, g = divmod(u, NG)
                if m == 0:
                    act.wait_ge(dt2_in[g // 2], 64 * (s.c + 1))
                wait(act, scan, s.c * UNITS + u - DA + 1)
                act.activation(da[:, u % DA, :], dt2[:, g, :], ACT.Exp, scale=a_neg[:, g, m:m + 1]
                               ).then_inc(da_set, 1)

            def times_b(c, par, n, j):
                if n == 0 and j == 0:
                    act.wait_ge(pT_set, c + 1)
                    act.wait_ge(hT_set[0], 2 * (c + 1))
                    act.wait_ge(hT_set[1], 2 * (c + 1))
                m, k = divmod(n, SP)
                wait(act, u_set, c * UNITS + NG * (m - XB + 1))
                act.mul(xb[:, m % XB, j, :, k, :], by_group(hT[par][:, j, :]), pT[par][:, j, n + 1:n + 2]
                        ).then_inc(xb_act, 1)

            def take_hT(s, j):
                act.wait_ge(a_full, s.a_count(f"hT{j}"))
                wait(act, xb_dve, NS * s.c)
                act.copy(hT[1 - s.par][:, j, :], a_ps[:, :]).then_inc(hT_set[1], 1)

            def take_xT(s, k):
                act.wait_ge(a_full, s.a_count(f"xT{k}"))
                act.activation(xnT[:, k, :], a_ps[:, :], ACT.Identity, scale=n_w[:, k:k + 1], bias=n_b[:, k:k + 1]
                               ).then_inc(xnT_set, 1)

            def take_in(s, db):
                if db == 0:
                    wait(act, halo, s.c + 1)
                    wait(act, dt_set, 3 * DB * (s.c + 1))
                    act.wait_ge(pool_set, 6)
                act.wait_ge(a_full, s.a_count(f"in{db}"))
                act.copy(hin[:, db, KC - 1:KC - 1 + T], a_ps[:, :]).then_inc(hin_set, 1)

            def silu_h(s):
                act.wait_ge(conv, KC * DB * (s.c + 2))
                act.activation(h[1 - s.par][:, :, :], h[1 - s.par][:, :, :], ACT.Silu).then_inc(h_set, 1)

            def softplus_exp(s):
                c = s.c
                act.wait_ge(z_set, DB * (c + 2))
                act.activation(ez[:, :, :], z[:, :, :], ACT.Abs).then_inc(soft, 1)
                act.wait_ge(soft, 3 * (c + 1) + 1)
                act.activation(ez[:, :, :], ez[:, :, :], ACT.Exp, scale=-1.0).then_inc(soft, 1)

            def softplus_ln(s):
                act.wait_ge(soft, 3 * (s.c + 1) + 2)
                act.activation(dt[:, :, :], ez[:, :, :], ACT.Ln, bias=1.0).then_inc(soft, 1)

            def silu_y(s):
                act.wait_ge(y_out, DB * s.c)
                act.activation(yv[:, :, :], yv[:, :, :], ACT.Silu).then_inc(y_silu, 1)

            def take_x1T(s, k):
                act.wait_ge(q_full, s.q_count(f"x1T{k}"))
                act.copy(x1T[:, k, :], q_ps[:, :]).then_inc(x1T_set, 1)

            def exp_logits(s):
                act.wait_ge(route, ROUTE * (s.c - 1) + 2)
                act.activation(ex[:, :, :], lg[:, :, :], ACT.Exp).then_inc(e_set, 1)

            def stages(s, u):
                whole = not s.scan
                for k in range(KD):
                    if s.a and (u == (11, 14)[k] or whole):
                        take_xT(s, k)
                if s.q and (u == 8 or whole):
                    silu_y(s)
                for db in range(DB):
                    if s.a and (u == 17 + 3 * db or whole):
                        take_in(s, db)
                if s.a and (u == 33 or whole):
                    silu_h(s)
                for k in range(KD):
                    if s.q and (u == (35, 37)[k] or whole):
                        take_x1T(s, k)
                if s.q and (u == 41 or whole):
                    exp_logits(s)
                if s.a and (u == 43 or whole):
                    softplus_exp(s)
                if s.a and (u == 47 or whole):
                    softplus_ln(s)
                for j in (1, 3):
                    if s.a and (u == 48 + 3 * (j // 2) or whole):
                        take_hT(s, j)

            def body(s):
                for u in range(UNITS if s.scan else 1):
                    if s.scan:
                        unit(s, u)
                    if s.scan and u % NG in (3, 4, 5):
                        m = u // NG + 1
                        for i in range(2):
                            k, j = divmod(2 * (u % NG - 3) + i, TJ - 1)
                            if m < NM:
                                times_b(s.c, s.par, SP * m + k, j)
                            elif s.a:
                                times_b(s.c + 1, 1 - s.par, k, j)
                    stages(s, u)
                if not s.scan and s.a:
                    for k in range(SP):
                        for j in range(TJ - 1):
                            times_b(0, 0, k, j)

            steps_of(act.Fori, body)

        @block.vector
        def _(dve):
            dve.wait_ge(params, 16 * N_PARAMS)
            dve.sem_inc(res, 1)
            dve.wait_ge(pool_set, 6)

            def times_b(c, par, n):
                m, k = divmod(n, SP)
                wait(dve, u_set, c * UNITS + NG * (m - XB + 1))
                if n == 0:
                    dve.wait_ge(hT_set[1], 2 * (c + 1))
                    dve.wait_ge(pT_set, c + 1)
                dve.tensor_scalar(xb[:, m % XB, TJ - 1, :, k, :], by_group(hT[par][:, TJ - 1, :]),
                                  pT[par][:, TJ - 1, n + 1:n + 2], None, ALU.mult).then_inc(xb_dve, 1)

            def run_scan(s, u):
                r, i = divmod(u, 4)
                t = s.c * UNITS + u
                dve.wait_ge(u_set, t + 1)
                dve.wait_ge(da_set, t + 1)
                wait(dve, prod_set, t - 7)
                if i == 0:
                    wait(dve, carried, s.c * (UNITS // 4) + r - 1)
                dve.tensor_tensor_scan(state[:, r % 2, i, :], da[:, u % DA, :], u_ps[:, u % 2, :],
                                       carry[:, u:u + 1], ALU.mult, ALU.add).then_inc(scan, 1)

            def keep_carry(s, r):
                dve.wait_ge(scan, s.c * UNITS + 4 * (r + 1))
                dve.tensor_copy(carry[:, 4 * r:4 * r + 4], state[:, r % 2, :, T - 1]).then_inc(carried, 1)

            def norm_x(s):
                c = s.c
                dve.wait_ge(x_in, 16 * (c + 2))
                for j in range(TJ):
                    i = dve.bn_stats(st_a[:, j, :], xt[:, j, :])
                i.then_inc(stat_a, 1)
                dve.wait_ge(stat_a, 3 * (c + 1) + 1)
                hold(dve, passed[2])
                for j in range(TJ):
                    i = dve.bn_aggr(mv_a[:, j, :], st_a[:, j, :])
                i.then_inc(stat_a, 1)

            def norm_x_end(s):
                c = s.c
                dve.wait_ge(stat_a, 3 * (c + 1) + 2)
                dve.wait_ge(rstd_a, 2 * (c + 2))
                wait(dve, xnT_set, 2 * (c + 1))
                for j in range(TJ):
                    i = dve.tensor_scalar(xn[:, j, :], xt[:, j, :], mv_a[:, j, 0:1], rs_a[:, j:j + 1],
                                          ALU.subtract, ALU.mult)
                i.then_inc(stat_a, 1)

            def conv_tap(s, db, k):
                c = s.c
                m = KC * DB * (c + 1) + KC * db + k
                w = conv_w[:, db, k:k + 1]
                cv = h[1 - s.par]
                if k == 0:
                    dve.wait_ge(hin_set, DB * (c + 1) + db + 1)
                    dve.tensor_scalar(cv[:, db, :], hin[:, db, 0:T], w, None, ALU.mult).then_inc(conv, 1)
                else:
                    dve.wait_ge(conv, m)
                    dve.scalar_tensor_tensor(out=cv[:, db, :], in0=hin[:, db, k:k + T], scalar=w, in1=cv[:, db, :],
                                             op0=ALU.mult, op1=ALU.add).then_inc(conv, 1)

            def move_halo(s):
                dve.wait_ge(conv, KC * DB * (s.c + 2))
                dve.tensor_copy(hin[:, :, 0:KC - 1], hin[:, :, T:T + KC - 1]).then_inc(halo, 1)

            def take_hT(s, j):
                dve.wait_ge(a_full, s.a_count(f"hT{j}"))
                wait(dve, xb_act, (TJ - 1) * NS * s.c)
                dve.tensor_copy(hT[1 - s.par][:, j, :], a_ps[:, :]).then_inc(hT_set[0], 1)

            def take_pT(s):
                dve.wait_ge(a_full, s.a_count("pT"))
                wait(dve, xb_act, (TJ - 1) * NS * s.c)
                dve.tensor_copy(pT[1 - s.par][:, :, :], a_ps[:, 0:TJ * (2 * NS + 1)].rearrange("p (j n) -> p j n", j=TJ)
                                ).then_inc(pT_set, 1)

            def take_rows(s):
                dve.wait_ge(a_full, s.a_count("rows"))
                wait(dve, c_out, 16 * (s.c + 1))
                dve.tensor_copy(bcf[:, :], a_ps[0:2 * NS + 1, :]).then_inc(rows_set, 1)

            def take_dt(s):
                c = s.c
                dve.wait_ge(a_full, s.a_count("dt"))
                dve.wait_ge(halo, c + 2)
                for db in range(DB):
                    i = dve.tensor_scalar(z[:, db, :], a_ps[:, :], dt_w[:, db:db + 1], dt_b[:, db:db + 1],
                                          ALU.mult, ALU.add).then_inc(z_set, 1)

            def finish_dt(s, db):
                c, d = s.c, dt
                k = DB * (c + 1) + db
                dve.wait_ge(soft, 3 * (c + 2))
                dve.tensor_scalar(small[:, db, :], ez[:, db, :], TINY, None, ALU.is_lt).then_inc(dt_set, 1)
                dve.wait_ge(dt_set, 3 * k + 1)
                dve.wait_ge(series, 2 * (2 * (c + 1) + db // 2 + 1))
                hold(dve, passed[2])
                dve.copy_predicated(d[:, db, :], small[:, db, :], ser[db // 2][:, db % 2, :]).then_inc(dt_set, 1)
                dve.wait_ge(dt_set, 3 * k + 2)
                dve.scalar_tensor_tensor(out=d[:, db, :], in0=z[:, db, :], scalar=0.0, in1=d[:, db, :],
                                         op0=ALU.max, op1=ALU.add).then_inc(dt_set, 1)

            def take_y(s, db):
                dve.wait_ge(summed, s.c * UNITS - NG + 2 * db + 2)
                if db == 0:
                    wait(dve, y_silu, s.c)
                dve.scalar_tensor_tensor(out=yv[:, db, :], in0=h[1 - s.par][:, db, :], scalar=d_skip[:, db:db + 1],
                                         in1=y_ps[:, db, :], op0=ALU.mult, op1=ALU.add).then_inc(y_out, 1)

            def residual(s, half):
                k = 1 + 5 * (s.c - 1)
                dve.wait_ge(q_full, s.q_count(f"op{half}"))
                if half == 0:
                    dve.wait_ge(xr_in, 16 * s.c)
                r = xr[:, 2 * half:2 * half + 2, :].rearrange("p a b -> p (a b)")
                dve.scalar_tensor_tensor(out=r, in0=r, scalar=2.0, in1=q_ps[:, :], op0=ALU.mult, op1=ALU.add
                                         ).then_inc(res, 1)
                dve.wait_ge(res, k + half + 1)

            def stats_q(s):
                k = 1 + 5 * (s.c - 1)
                for j in range(TJ):
                    i = dve.bn_stats(st_q[:, j, :], xr[:, j, :])
                i.then_inc(res, 1)
                dve.wait_ge(res, k + 3)
                hold(dve, passed[2])
                for j in range(TJ):
                    i = dve.bn_aggr(mv_q[:, j, :], st_q[:, j, :])
                i.then_inc(res, 1)

            def norm_q(s):
                c = s.c
                dve.wait_ge(res, 1 + 5 * (c - 1) + 4)
                dve.wait_ge(rstd_q, 2 * c)
                dve.wait_ge(x1_out, 1 + 16 * (c - 1))
                dve.wait_ge(slotted, 16 * (ZEROS + TOPK * TJ * (c - 1)))
                dve.wait_ge(blanked, 16 * BLANKS)
                for j in range(TJ):
                    i = dve.tensor_scalar(x1[:, j, 0:D], xr[:, j, :], mv_q[:, j, 0:1], rs_q[:, j:j + 1],
                                          ALU.subtract, ALU.mult)
                i.then_inc(res, 1)

            def over_e(a):
                return a.unsqueeze(2).to_broadcast([P, TJ, E])

            def routing(s, part):
                c = s.c
                n = [{0: 0, 1: 2, 2: 20}[part]]
                r0 = ROUTE * (c - 1)

                def done(i):
                    n[0] += 1
                    i.then_inc(route, 1)
                    dve.wait_ge(route, r0 + n[0])

                if part == 0:
                    dve.wait_ge(q_full, s.q_count("rt"))
                    logits = q_ps[:, 0:TJ * E].rearrange("p (j e) -> p j e", e=E)
                    done(dve.tensor_reduce(mx[:, :], logits, AX.X, ALU.max))
                    done(dve.tensor_tensor(lg[:, :, :], logits, over_e(mx[:, :]), ALU.subtract))
                if part == 1:
                    dve.wait_ge(e_set, c)
                    done(dve.tensor_reduce(su[:, :], ex[:, :, :], AX.X, ALU.add))
                    done(dve.reciprocal(rsu[:, :], su[:, :]))
                    done(dve.tensor_tensor(pr[:, :, :], ex[:, :, :], over_e(rsu[:, :]), ALU.mult))
                    src = pr
                    for k in range(TOPK):
                        done(dve.tensor_reduce(pk[:, k, :], src[:, :, :], AX.X, ALU.max))
                        done(dve.tensor_tensor(eq[:, :, :], src[:, :, :], over_e(pk[:, k, :]), ALU.is_equal))
                        done(dve.tensor_tensor(wr[:, :, :], eq[:, :, :], rank, ALU.mult))
                        done(dve.tensor_reduce(wm[:, :], wr[:, :, :], AX.X, ALU.max))
                        done(dve.tensor_tensor(oh[:, k, :, :], wr[:, :, :], over_e(wm[:, :]), ALU.is_equal))
                        if k == 0:
                            done(dve.scalar_tensor_tensor(
                                out=pr2[:, :, :].rearrange("p a b -> p (a b)"),
                                in0=oh[:, 0, :, :].rearrange("p a b -> p (a b)"), scalar=-2.0,
                                in1=pr[:, :, :].rearrange("p a b -> p (a b)"), op0=ALU.mult, op1=ALU.add))
                            src = pr2
                    done(dve.tensor_tensor(hot_before[:, :], hot_before[:, :], hot_sum[:, :], ALU.add))
                    done(dve.tensor_tensor(hot[:, :, :], oh[:, 0, :, :], oh[:, 1, :, :], ALU.add))
                    done(dve.tensor_reduce(hot_sum[:, :], hot[:, :, :].rearrange("p j e -> p e j"), AX.X, ALU.add))
                    done(dve.tensor_tensor(den[:, :], pk[:, 0, :], pk[:, 1, :], ALU.add))
                if part == 2:
                    posn = q_ps[:, 0:TJ * E].rearrange("p (j e) -> p j e", e=E)
                    ohf = oh[:, :, :, :].rearrange("p k j e -> p (k j) e")
                    dve.wait_ge(q_full, s.q_count("pos"))
                    done(dve.tensor_tensor(po[:, 0:TJ, :], oh[:, 0, :, :], posn, ALU.mult))
                    done(dve.tensor_tensor(po[:, TJ:2 * TJ, :], oh[:, 1, :, :], posn, ALU.mult))
                    done(dve.tensor_reduce(pos_k[:, :], po[:, :, :], AX.X, ALU.add))
                    done(dve.tensor_tensor(bo[:, :, :], ohf, base8, ALU.mult))
                    done(dve.tensor_reduce(base_k[:, :], bo[:, :, :], AX.X, ALU.add))
                    done(dve.tensor_scalar(keep[:, :], pos_k[:, :], float(CAP), None, ALU.is_lt))
                    done(dve.reciprocal(rden[:, :], den[:, :]))
                    done(dve.tensor_tensor(gk[:, :, :], pk[:, :, :],
                                           rden[:, :].unsqueeze(1).to_broadcast([P, TOPK, TJ]), ALU.mult))
                    done(dve.tensor_tensor(gates[:, bass.ds((c - 1) * 8, 8)], gk[:, :, :].rearrange("p k j -> p (k j)"),
                                           keep[:, :], ALU.mult))
                    done(dve.tensor_tensor(kpos[:, :], keep[:, :], pos_k[:, :], ALU.mult))
                    trash = cst[:, bass.ds((c - 1) * 8 + C_TRASH, 8)]
                    done(dve.tensor_tensor(kpos[:, :], kpos[:, :], base_k[:, :], ALU.add))
                    done(dve.tensor_tensor(far[:, :], kpos[:, :], trash, ALU.subtract))
                    done(dve.tensor_tensor(far[:, :], far[:, :], keep[:, :], ALU.mult))
                    done(dve.tensor_tensor(sidx[:, :], far[:, :], trash, ALU.add))
                    hold(dve, passed[2])
                    done(dve.tensor_copy(x1[:, :, D], cst[:, bass.ds((c - 1) * 8 + C_TRASH, TJ)]))
                    done(dve.tensor_copy(x1[:, :, D + 1], base_k[:, 0:TJ]))
                    assert n[0] == ROUTE

            def stages(s, u):
                whole = not s.scan
                if s.a and (u == 2 or whole):
                    norm_x(s)
                for db in range(DB):
                    if s.q and (u == 1 + db or whole):
                        take_y(s, db)
                if s.a and (u == 5 or whole):
                    norm_x_end(s)
                if s.q and (u == 13 or whole):
                    residual(s, 0)
                for db in range(DB):
                    for k in range(KC):
                        if s.a and (u == 14 + 4 * db + k or whole):
                            conv_tap(s, db, k)
                if s.q and (u == 25 or whole):
                    residual(s, 1)
                    stats_q(s)
                if s.q and (u == 29 or whole):
                    norm_q(s)
                if s.a and (u == 31 or whole):
                    move_halo(s)
                if s.a and (u == 33 or whole):
                    take_rows(s)
                if s.a and (u == 35 or whole):
                    take_dt(s)
                if s.q and (u == 38 or whole):
                    routing(s, 0)
                if s.a and (u == 38 or whole):
                    take_pT(s)
                if s.q and (u == 40 or whole):
                    routing(s, 1)
                if s.a and (u == 42 or whole):
                    take_hT(s, 0)
                if s.q and (u == 44 or whole):
                    routing(s, 2)
                if s.a and (u == 49 or whole):
                    take_hT(s, 2)
                for db in range(DB):
                    if s.a and (u == 47 + db or whole):
                        finish_dt(s, db)

            def body(s):
                if not s.scan:
                    stages(s, 0)
                    if s.a:
                        times_b(0, 0, 0)
                        times_b(0, 0, 1)
                    return
                for u in range(UNITS):
                    run_scan(s, u)
                    if u % 4 == 1 and u > 4:
                        keep_carry(s, u // 4 - 1)
                    if u % NG in (2, 3):
                        m, k = u // NG + 1, u % NG - 2
                        if m < NM:
                            times_b(s.c, s.par, SP * m + k)
                        elif s.a:
                            times_b(s.c + 1, 1 - s.par, k)
                    stages(s, u)
                keep_carry(s, UNITS // 4 - 1)

            steps_of(dve.Fori, body)

        @block.tensor
        def _(pe):
            pe.wait_ge(params, 16 * N_PARAMS)

            def turn_b(c, u):
                m, g = divmod(u, NG)
                if g == 0:
                    pe.wait_ge(xb_act, (TJ - 1) * (NS * c + SP * (m + 1)))
                    pe.wait_ge(xb_dve, NS * c + SP * (m + 1))
                wait(pe, scan, c * UNITS + u - 1)
                for j in range(TJ):
                    i = pe.transpose(u_ps[:, u % 2, j * P:(j + 1) * P],
                                     xb[:, m % XB, j, g, :, :].rearrange("p s c -> p (s c)"), ident)
                i.then_inc(u_set, 1)

            def add_up(c, u):
                m, g = divmod(u, NG)
                db = g // 2
                pe.wait_ge(prod_set, c * UNITS + u + 2)
                if m == 0:
                    wait(pe, y_out, DB * (c - 1) + db + 1)
                for half in range(2):
                    pe.matmul(y_ps[half * GC:(half + 1) * GC, db, :], both, prod[:, (u + half) % PR, :],
                              start=(m == 0), stop=(m == NM - 1)).then_inc(summed, 1)

            def take_bank(s, use):
                k = int(use[-1]) if use[-1].isdigit() else 0
                before = {
                    "xT0": (hT_set[1], 2 * (s.c + 1)),
                    "xT1": (xnT_set, KD * (s.c + 1) + 1), "in0": (xnT_set, KD * (s.c + 2)),
                    "in": (hin_set, DB * (s.c + 1) + k), "rows": (hin_set, DB * (s.c + 2)),
                    "dt": (rows_set, s.c + 2), "pT": (z_set, DB * (s.c + 2)), "hT0": (pT_set, s.c + 2),
                    "hT1": (hT_set[0], 2 * (s.c + 1) + 1), "hT2": (hT_set[1], 2 * (s.c + 1) + 1),
                    "hT3": (hT_set[0], 2 * (s.c + 2)),
                    "op1": (res, 1 + 5 * (s.c - 1) + 1), "x1T0": (res, 1 + 5 * (s.c - 1) + 2),
                    "x1T1": (x1T_set, KD * (s.c - 1) + 1), "rt": (x1T_set, KD * s.c),
                    "pos": (route, ROUTE * (s.c - 1) + 2),
                }
                key = use if use in before else use[:-1]
                if key in before:
                    wait(pe, *before[key])

            def xT(s, k):
                if k == 0:
                    pe.wait_ge(stat_a, 3 * (s.c + 2))
                take_bank(s, f"xT{k}")
                for j in range(TJ):
                    i = pe.transpose(a_ps[:, j * P:(j + 1) * P], xn[:, j, k * P:(k + 1) * P], ident)
                i.then_inc(a_full, 1)

            def in_proj(s, db, k):
                if k == 0:
                    take_bank(s, f"in{db}")
                i = pe.matmul(a_ps[:, :], w_in[:, k, db * P:(db + 1) * P], xnT[:, k, :],
                              start=(k == 0), stop=(k == KD - 1))
                if k == KD - 1:
                    i.then_inc(a_full, 1)

            def turn_h(s, j):
                take_bank(s, f"hT{j}")
                for db in range(DB):
                    i = pe.transpose(a_ps[:, db * P:(db + 1) * P], h[1 - s.par][:, db, j * P:(j + 1) * P], ident)
                i.then_inc(a_full, 1)

            def x_proj(s, half):
                if half == 0:
                    pe.wait_ge(h_set, s.c + 2)
                    take_bank(s, "rows")
                for db in range(2 * half, 2 * half + 2):
                    i = pe.matmul(a_ps[0:2 * NS + 1, :], w_x[:, db, :], h[1 - s.par][:, db, :],
                                  start=(db == 0), stop=(db == DB - 1))
                if half == 1:
                    i.then_inc(a_full, 1)

            def turn_rows(s):
                w = 2 * NS + 1
                take_bank(s, "pT")
                hold(pe, passed[3])
                for j in range(TJ):
                    i = pe.transpose(a_ps[:, j * w:(j + 1) * w], bcf[:, j * P:(j + 1) * P], ident[0:w, 0:w])
                i.then_inc(a_full, 1)

            def spread_dt(s):
                take_bank(s, "dt")
                pe.matmul(a_ps[:, :], ones[0:1, :], bcf[0:1, :], start=True, stop=True).then_inc(a_full, 1)

            def out_proj(s, half, part):
                if half == 0 and part == 0:
                    pe.wait_ge(y_silu, 1 + s.c)
                if part == 0:
                    take_bank(s, f"op{half}")
                jj, pair = divmod(part, 2)
                j = 2 * half + jj
                for db in range(2 * pair, 2 * pair + 2):
                    i = pe.matmul(q_ps[:, jj * D:(jj + 1) * D], yv[:, db, j * P:(j + 1) * P], w_out[:, db, :],
                                  start=(db == 0), stop=(db == DB - 1))
                if part == 3:
                    i.then_inc(q_full, 1)

            def x1_T(s, k):
                if k == 0:
                    pe.wait_ge(res, 1 + 5 * s.c)
                take_bank(s, f"x1T{k}")
                for j in range(TJ):
                    i = pe.transpose(q_ps[:, j * P:(j + 1) * P], x1[:, j, k * P:(k + 1) * P], ident)
                i.then_inc(q_full, 1)

            def router(s):
                pe.wait_ge(x1T_set, 2 * s.c)
                take_bank(s, "rt")
                for j in range(TJ):
                    for k in range(KD):
                        i = pe.matmul(q_ps[:, j * E:(j + 1) * E], x1T[:, k, j * P:(j + 1) * P], w_r[:, k, :],
                                      start=(k == 0), stop=(k == KD - 1))
                i.then_inc(q_full, 1)

            def positions(s):
                pe.wait_ge(route, ROUTE * (s.c - 1) + 20)
                take_bank(s, "pos")
                for j in range(TJ):
                    o = q_ps[:, j * E:(j + 1) * E]
                    pe.matmul(o, tri, hot[:, j, :], start=True, stop=False)
                    for i in range(j):
                        pe.matmul(o, ones, hot[:, i, :], start=False, stop=False)
                    last = pe.matmul(o, ones, hot_before[:, :], start=False, stop=True)
                last.then_inc(q_full, 1)

            def stages(s, u):
                whole = not s.scan
                for k in range(KD):
                    if s.a and (u == (4, 7)[k] or whole):
                        xT(s, k)
                for part in range(4):
                    if s.q and (u == (6, 7, 8, 10)[part] or whole):
                        out_proj(s, 0, part)
                for db in range(DB):
                    for k in range(KD):
                        if s.a and (u == 10 + 3 * db + k or whole):
                            in_proj(s, db, k)
                for part in range(4):
                    if s.q and (u == (13, 16, 20, 22)[part] or whole):
                        out_proj(s, 1, part)
                for k in range(KD):
                    if s.q and (u == (28, 31)[k] or whole):
                        x1_T(s, k)
                for half in range(2):
                    if s.a and (u == 29 + half or whole):
                        x_proj(s, half)
                if s.q and (u == 33 or whole):
                    router(s)
                if s.a and (u == 32 or whole):
                    spread_dt(s)
                if s.a and (u == 34 or whole):
                    turn_rows(s)
                for j in range(TJ):
                    if s.a and (u == (39, 42, 46, 47)[j] or whole):
                        turn_h(s, j)
                if s.q and (u == 39 or whole):
                    positions(s)

            def body(s):
                ahead = 3
                if not s.scan:
                    if s.q:
                        add_up(s.c - 1, UNITS - 2)
                    stages(s, 0)
                    if s.a:
                        for u in range(ahead):
                            turn_b(0, u)
                    return
                for u in range(0, UNITS, 2):
                    for v in (u, u + 1):
                        if v + ahead < UNITS:
                            turn_b(s.c, v + ahead)
                        elif s.a:
                            turn_b(s.c + 1, v + ahead - UNITS)
                        if v > u and u > 0:
                            add_up(s.c, u - 2)
                        elif v > u and s.q:
                            add_up(s.c - 1, UNITS - 2)
                        stages(s, v)

            steps_of(pe.Fori, body)


def experts(nc, io, scr, x1, x1_in):
    with ExitStack() as ctx:
        def sb(name, shape, dt=F32):
            return ctx.enter_context(nc.sbuf_tensor(name, shape, dt))

        def sem(name):
            return ctx.enter_context(nc.semaphore(name))

        HALF = CAP // 2
        AIM = 7
        PASSES = ((0, 0), (0, 1), (1, 0))
        XG = KD * CT // 4
        HG = 2 * HB

        ident = sb("ident2", [P, P])
        b1 = sb("b1", [P, HB, E])
        b2 = sb("b2", [P, E, D])
        rows = [sb(f"rows{i}", [P, CT, DX]) for i in range(2)]
        bases = sb("bases", [P, E])
        spare = sb("spare", [P, CT])
        first = sb("first", [P, CT])
        real = sb("real", [P, CT])
        dest = sb("dest", [P, CT])
        dest_u = sb("dest_u", [P, CT], U32)
        xT = [sb(f"xT_{n}", [P, KD * CAP], F32R) for n in ("hi", "lo")]
        w1_raw = sb("w1_raw", [P, KD, H])
        w2_raw = sb("w2_raw", [P, HB, D])
        w1 = [[sb(f"w1_{n}{i}", [P, KD, H], F32R) for n in ("hi", "lo")] for i in range(2)]
        w2 = [[sb(f"w2_{n}{i}", [P, HB, D], F32R) for n in ("hi", "lo")] for i in range(2)]
        b1_e = sb("b1_e", [P, 2, HB])
        relu = sb("relu", [P, 4, HALF])
        hid = [sb(f"hid_{n}", [P, HB, CAP], F32R) for n in ("hi", "lo")]
        eo = sb("eo", [P, CT, D])
        x_ps = ctx.enter_context(nc.psum_tensor("x_ps", [P, 2, 512], F32))
        h_ps = ctx.enter_context(nc.psum_tensor("h_ps", [P, 4, 512], F32))
        o_ps = ctx.enter_context(nc.psum_tensor("o_ps", [P, 2, 512], F32))

        params = sem("params2")
        rows_in = [sem("rows_in0"), sem("rows_in1")]
        ident_in = sem("ident_in")
        w_in = [sem("w1_in"), sem("w2_in")]
        b1_set = sem("b1_set")
        w_hi = [sem("w1_hi_set"), sem("w2_hi_set")]
        w_lo = [sem("w1_lo_set"), sem("w2_lo_set")]
        x_tr = sem("x_tr")
        x_hi = sem("x_hi")
        x_lo = sem("x_lo")
        h_mm = sem("h_mm")
        h_relu = sem("h_relu")
        h_hi = sem("h_hi")
        h_lo = [sem("h_lo_even"), sem("h_lo_odd")]
        o_mm = sem("o_mm")
        o_set = sem("o_set")
        o_out = sem("o_out")
        aimed = sem("aimed")
        passed = [sem("passed_sp2"), sem("passed_pool2")]

        block = ctx.enter_context(nc.Block())

        def over_experts(engine_loop, body):
            body(0, 0, True)
            with engine_loop(1, E - 2, 2) as e:
                body(e, 1, True)
                body(e + 1, 0, True)
            body(E - 1, 1, False)

        @block.sync
        def _(sp):
            def load_rows(e, par):
                sp.dma_start(rows[par][:, :, :], scr["expert_in"][bass.ds(e * CAP, CAP), :]
                             .rearrange("(j p) d -> p j d", p=P)).then_inc(rows_in[par], 16)

            def load_weights(e):
                sp.dma_start(w1_raw[:, :, :], io["w1"][bass.ds(e * D, D), :].rearrange("(k p) n -> p k n", p=P)
                             ).then_inc(w_in[0], 16)
                sp.dma_start(w2_raw[:, :, :], io["w2"][bass.ds(e * H, H), :].rearrange("(k p) n -> p k n", p=P)
                             ).then_inc(w_in[1], 16)

            def body(e, par):
                sp.wait_ge(aimed, AIM * (e + 1))
                hold(sp, passed[0])
                sp.wait_ge(x_tr, XG * (e + 1))
                hold(sp, passed[0])
                load_rows(e + 2, par)
                sp.wait_ge(w_lo[0], e + 2)
                hold(sp, passed[0])
                sp.wait_ge(w_lo[1], e + 2)
                load_weights(e + 2)

            sp.dma_start(ident[:, :], io["consts"][:, C_ID:C_ID + P]).then_inc(ident_in, 16)
            load_rows(0, 0)
            load_weights(0)
            sp.dma_start(bases[:, :], io["consts"][:, C_BASE:C_BASE + E]).then_inc(params, 16)
            sp.dma_start(spare[:, :], io["consts"][:, C_SPARE:C_SPARE + CT]).then_inc(params, 16)
            sp.dma_start(b1[:, :, :], io["b1"]).then_inc(params, 16)
            sp.dma_start(b2[:, :, :], io["b2"].partition_broadcast(P)).then_inc(params, 16)
            load_rows(1, 1)
            sp.wait_ge(w_lo[0], 1)
            sp.wait_ge(w_lo[1], 1)
            load_weights(1)
            body(0, 0)
            with sp.Fori(1, E - 4, 2) as e:
                body(e, 1)
                body(e + 1, 0)
            body(E - 3, 1)
            for c in range(NC):
                sp.dma_start(x1[:, c, :, :], scr["x1"][c * T:(c + 1) * T, :].rearrange("(j p) d -> p j d", p=P)
                             ).then_inc(x1_in, 16)

        @block.gpsimd
        def _(pool):
            def low_weights(e, par, k):
                w, raw = ((w1, w1_raw), (w2, w2_raw))[k]
                pool.wait_ge(w_hi[k], e + 1)
                pool.tensor_tensor(w[par][1][:, :, :], raw[:, :, :], w[par][0][:, :, :].bitcast(F32), ALU.subtract
                                   ).then_inc(w_lo[k], 1)

            def body(e, par, more):
                for hb in range(HB):
                    pool.wait_ge(h_hi, HG * e + 2 * hb + 1)
                    pool.tensor_tensor(hid[1][:, hb, 0:HALF], relu[:, 2 * hb % 4, :],
                                       hid[0][:, hb, 0:HALF].bitcast(F32), ALU.subtract).then_inc(h_lo[0], 1)
                if more:
                    low_weights(e + 1, 1 - par, 0)
                    low_weights(e + 1, 1 - par, 1)
                for j in range(CT):
                    pool.wait_ge(aimed, AIM * (e + 1))
                    pool.wait_ge(o_set, CT * e + j + 1)
                    hold(pool, passed[1])
                    pool.indirect_dma_start(scr["choice_out"][:, :], bass.IndirectOffsetOnAxis(dest_u[:, j:j + 1], 0),
                                            eo[:, j, :], None).then_inc(o_out, 16)

            low_weights(0, 0, 1)
            over_experts(pool.Fori, body)
            pool.wait_ge(o_out, 16 * CT * E)

        @block.scalar
        def _(act):
            def high_weights(e, par, k):
                act.wait_ge(w_in[k], 16 * (e + 1))
                wait(act, o_mm, CT * (e - 1))
                w, raw = ((w1, w1_raw), (w2, w2_raw))[k]
                act.copy(w[par][0][:, :, :], raw[:, :, :]).then_inc(w_hi[k], 1)

            def high_x(e, par):
                wait(act, h_mm, HG * e)
                for g in range(XG):
                    act.wait_ge(x_tr, XG * e + g + 1)
                    act.copy(xT[0][:, g * 512:(g + 1) * 512], x_ps[:, (par + g) % 2, :]).then_inc(x_hi, 1)

            def body(e, par, more):
                act.copy(b1_e[:, par, :], b1[:, :, bass.ds(e, 1)].rearrange("p h o -> p (h o)")).then_inc(b1_set, 1)
                act.wait_ge(b1_set, e + 1)
                for g in range(HG):
                    hb, half = divmod(g, 2)
                    act.wait_ge(h_mm, HG * e + g + 1)
                    wait(act, h_lo[half], HB * e + hb - 1)
                    act.activation(relu[:, g % 4, :], h_ps[:, g % 4, 0:HALF], ACT.Relu, bias=b1_e[:, par, hb:hb + 1]
                                   ).then_inc(h_relu, 1)
                    if more and g in (3, 9):
                        high_weights(e + 1, 1 - par, g // 9)
                if more:
                    high_x(e + 1, 1 - par)

            high_x(0, 0)
            high_weights(0, 0, 0)
            act.wait_ge(params, 64)
            high_weights(0, 0, 1)
            over_experts(act.Fori, body)

        @block.vector
        def _(dve):
            def low_x(e, par):
                wait(dve, h_mm, HG * e)
                for g in range(XG):
                    cols = slice(g * 512, (g + 1) * 512)
                    dve.wait_ge(x_hi, XG * e + g + 1)
                    dve.tensor_tensor(xT[1][:, cols], x_ps[:, (par + g) % 2, :], xT[0][:, cols].bitcast(F32),
                                      ALU.subtract).then_inc(x_lo, 1)

            def aim(e, par):
                n = [0]

                def done(i):
                    n[0] += 1
                    i.then_inc(aimed, 1)
                    dve.wait_ge(aimed, AIM * e + n[0])

                code = rows[par][:, :, D]
                done(dve.tensor_tensor(first[:, :], rows[par][:, :, D + 1],
                                       bases[:, bass.ds(e, 1)].to_broadcast([P, CT]), ALU.is_equal))
                done(dve.tensor_scalar(real[:, :], code, 0.0, None, ALU.is_gt))
                done(dve.tensor_scalar(dest[:, :], code, float(1 - SLOTS), None, ALU.add))
                done(dve.tensor_tensor(dest[:, :], dest[:, :], first[:, :], ALU.subtract))
                done(dve.tensor_tensor(dest[:, :], dest[:, :], spare[:, :], ALU.subtract))
                done(dve.tensor_tensor(dest[:, :], dest[:, :], real[:, :], ALU.mult))
                wait(dve, o_out, 16 * CT * e)
                done(dve.tensor_tensor(dest_u[:, :], dest[:, :], spare[:, :], ALU.add))
                assert n[0] == AIM

            def body(e, par, more):
                dve.wait_ge(rows_in[par], 8 * (e - par) + 16)
                wait(dve, o_mm, CT * e)
                for g in range(HG):
                    hb, half = divmod(g, 2)
                    cols = slice(half * HALF, (half + 1) * HALF)
                    dve.wait_ge(h_relu, HG * e + g + 1)
                    dve.tensor_copy(hid[0][:, hb, cols], relu[:, g % 4, :]).then_inc(h_hi, 1)
                    if half == 1:
                        dve.wait_ge(h_hi, HG * e + g + 1)
                        dve.tensor_tensor(hid[1][:, hb, cols], relu[:, g % 4, :], hid[0][:, hb, cols].bitcast(F32),
                                          ALU.subtract).then_inc(h_lo[1], 1)
                if more:
                    low_x(e + 1, 1 - par)
                aim(e, par)
                for j in range(CT):
                    dve.wait_ge(o_mm, CT * e + j + 1)
                    if j % 3 == 0:
                        wait(dve, o_out, 16 * CT * e)
                    dve.tensor_tensor(eo[:, j, :], o_ps[:, j % 2, 0:D],
                                      b2[:, bass.ds(e, 1), :].rearrange("p o d -> p (o d)"), ALU.add).then_inc(o_set, 1)

            low_x(0, 0)
            dve.wait_ge(w_hi[0], 1)
            dve.tensor_tensor(w1[0][1][:, :, :], w1_raw[:, :, :], w1[0][0][:, :, :].bitcast(F32), ALU.subtract
                              ).then_inc(w_lo[0], 1)
            dve.wait_ge(params, 64)
            over_experts(dve.Fori, body)

        @block.tensor
        def _(pe):
            pe.wait_ge(ident_in, 16)

            def turn(e, par):
                pe.wait_ge(rows_in[par], 8 * (e - par) + 16)
                for g in range(XG):
                    wait(pe, x_lo, XG * e + g - 1)
                    for i in range(4):
                        k, j = divmod(4 * g + i, CT)
                        last = pe.transpose(x_ps[:, (par + g) % 2, i * P:(i + 1) * P], rows[par][:, j, k * P:(k + 1) * P],
                                            ident[:, :])
                    last.then_inc(x_tr, 1)

            def hidden(e, par):
                pe.wait_ge(x_lo, XG * (e + 1))
                pe.wait_ge(w_lo[0], e + 1)
                for g in range(HG):
                    hb, half = divmod(g, 2)
                    wait(pe, h_relu, HG * e + g - 3)
                    n = 0
                    for a, b in PASSES:
                        for k in range(KD):
                            c0 = k * CAP + half * HALF
                            last = pe.matmul(h_ps[:, g % 4, 0:HALF], w1[par][a][:, k, hb * P:(hb + 1) * P],
                                             xT[b][:, c0:c0 + HALF], start=(n == 0), stop=(n == 3 * KD - 1))
                            n += 1
                    last.then_inc(h_mm, 1)

            def outputs(e, par):
                pe.wait_ge(h_lo[0], HB * (e + 1))
                pe.wait_ge(h_lo[1], HB * (e + 1))
                pe.wait_ge(w_lo[1], e + 1)
                for j in range(CT):
                    wait(pe, o_set, CT * e + j - 1)
                    n = 0
                    for a, b in PASSES:
                        for hb in range(HB):
                            last = pe.matmul(o_ps[:, j % 2, 0:D], hid[a][:, hb, j * P:(j + 1) * P], w2[par][b][:, hb, :],
                                             start=(n == 0), stop=(n == 3 * HB - 1))
                            n += 1
                    last.then_inc(o_mm, 1)

            def body(e, par, more):
                hidden(e, par)
                if more:
                    turn(e + 1, 1 - par)
                outputs(e, par)

            turn(0, 0)
            over_experts(pe.Fori, body)


def combine(nc, scr, gates, x1, x1_in, out):
    with ExitStack() as ctx:
        def sb(name, shape, dt=F32):
            return ctx.enter_context(nc.sbuf_tensor(name, shape, dt))

        def sem(name):
            return ctx.enter_context(nc.semaphore(name))

        got = sb("got", [P, NC, TJ, TOPK, D])
        st = sb("st_f", [P, NC, TJ, 6])
        mv = sb("mv_f", [P, NC, TJ, 2])
        ve = sb("ve_f", [P, NC, TJ])
        sd = sb("sd_f", [P, NC, TJ])
        rs = sb("rs_f", [P, NC, TJ])
        shift = sb("shift_f", [P, NC, TJ])

        rows_in = [sem(f"got{c}") for c in range(NC)]
        gated = sem("gated")
        added = sem("added")
        mixed = sem("mixed")
        rooted = sem("rooted")
        scaled = sem("scaled")
        normed = sem("normed")
        stored = sem("stored")

        block = ctx.enter_context(nc.Block())

        @block.sync
        def _(sp):
            for c in range(NC):
                sp.dma_start(got[:, c, :, :, :], scr["choice_out"][TOPK * c * T:TOPK * (c + 1) * T, :]
                             .rearrange("(j p k) d -> p j k d", p=P, k=TOPK)).then_inc(rows_in[c], 16)
            with sp.Fori(0, NC) as c:
                sp.wait_ge(normed, c + 1)
                sp.dma_start(out[bass.ds(c * T, T), :].rearrange("(j p) d -> p j d", p=P),
                             x1[:, bass.ds(c, 1), :, :].rearrange("p o j d -> p (o j) d")).then_inc(stored, 16)
            sp.wait_ge(stored, 16 * NC)

        @block.scalar
        def _(act):
            def root(c):
                act.wait_ge(mixed, 4 * c + 4)
                act.activation(sd[:, c, :], ve[:, c, :], ACT.Sqrt).then_inc(rooted, 1)

            def norm(c):
                act.wait_ge(scaled, 2 * c + 2)
                for j in range(TJ):
                    i = act.activation(x1[:, c, j, :], x1[:, c, j, :], ACT.Identity, scale=rs[:, c, j:j + 1],
                                       bias=shift[:, c, j:j + 1])
                i.then_inc(normed, 1)

            def first_choice(c):
                act.wait_ge(rows_in[c], 16)
                for j in range(TJ):
                    col = c * TOPK * TJ + j
                    i = act.mul(got[:, c, j, 0, :], got[:, c, j, 0, :], gates[:, col:col + 1])
                i.then_inc(gated, 1)

            for c in range(2):
                first_choice(c)
            for c in range(NC):
                root(c)
                if c + 2 < NC:
                    first_choice(c + 2)
                if c > 0:
                    norm(c - 1)
            norm(NC - 1)

        @block.gpsimd
        def _(pool):
            for c in range(NC):
                if c == 0:
                    pool.wait_ge(x1_in, 16 * NC)
                pool.wait_ge(gated, c + 1)
                pool.tensor_tensor(x1[:, c, :, :], x1[:, c, :, :], got[:, c, :, 0, :], ALU.add).then_inc(added, 1)

        @block.vector
        def _(dve):
            def mix(c):
                dve.wait_ge(rows_in[c], 16)
                dve.wait_ge(added, c + 1)
                for j in range(TJ):
                    col = (c * TOPK + 1) * TJ + j
                    i = dve.scalar_tensor_tensor(out=x1[:, c, j, :], in0=got[:, c, j, 1, :],
                                                 scalar=gates[:, col:col + 1], in1=x1[:, c, j, :],
                                                 op0=ALU.mult, op1=ALU.add)
                i.then_inc(mixed, 1)
                dve.wait_ge(mixed, 4 * c + 1)
                for j in range(TJ):
                    i = dve.bn_stats(st[:, c, j, :], x1[:, c, j, :])
                i.then_inc(mixed, 1)
                dve.wait_ge(mixed, 4 * c + 2)
                for j in range(TJ):
                    i = dve.bn_aggr(mv[:, c, j, :], st[:, c, j, :])
                i.then_inc(mixed, 1)
                dve.wait_ge(mixed, 4 * c + 3)
                dve.tensor_scalar(ve[:, c, :], mv[:, c, :, 1], EPS, None, ALU.add).then_inc(mixed, 1)

            def scale(c):
                dve.wait_ge(rooted, c + 1)
                dve.reciprocal(rs[:, c, :], sd[:, c, :]).then_inc(scaled, 1)
                dve.wait_ge(scaled, 2 * c + 1)
                dve.scalar_tensor_tensor(out=shift[:, c, :], in0=mv[:, c, :, 0], scalar=-1.0, in1=rs[:, c, :],
                                         op0=ALU.mult, op1=ALU.mult).then_inc(scaled, 1)

            for c in range(NC):
                mix(c)
                if c > 0:
                    scale(c - 1)
            scale(NC - 1)


def program(nc, io, out):
    scr = {
        "expert_in": nc.dram_tensor("expert_in", (SLOTS + TOPK * L, DX), F32, kind="Internal").ap(),
        "choice_out": nc.dram_tensor("choice_out", (TOPK * L + CAP, D), F32, kind="Internal").ap(),
        "x1": nc.dram_tensor("x1_scratch", (L, D), F32, kind="Internal").ap(),
        "c": nc.dram_tensor("c_scratch", (NS, L), F32, kind="Internal").ap(),
    }
    with nc.sbuf_tensor("gates", [P, TOPK * L // P], F32) as gates:
        mixer_and_routing(nc, io, scr, gates)
        with nc.sbuf_tensor("x1_all", [P, NC, TJ, D], F32) as x1, nc.semaphore("x1_in") as x1_in:
            experts(nc, io, scr, x1, x1_in)
            combine(nc, scr, gates, x1, x1_in, out)


def constants():
    import numpy as np

    c = np.zeros((P, C_END), np.float32)
    c[:, C_ID:C_ID + P] = np.eye(P)
    c[:, C_TRI:C_TRI + P] = np.triu(np.ones((P, P)), 1)
    c[:, C_ONE:C_ONE + P] = 1
    c[:, C_SPARE:C_SPARE + CT] = TOPK * L + np.arange(CAP).reshape(CT, P).T
    c[:, C_PAIR:C_PAIR + GC] = np.tile(np.eye(GC), (SP, 1))
    c[:, C_RANK:C_RANK + TJ * E] = np.tile(E - np.arange(E), TJ)
    c[:, C_BASE:C_BASE + TOPK * TJ * E] = np.tile(CAP * np.arange(E), TOPK * TJ)
    for ch in range(NC):
        for k in range(TOPK):
            for j in range(TJ):
                t = ch * T + j * P + np.arange(P)
                c[:, C_TRASH + (ch * TOPK + k) * TJ + j] = SLOTS + TOPK * t + k
    return c


def kernel(**inputs):
    import numpy as np
    import concourse.bacc as bacc
    from concourse.bass_utils import run_bass_kernel_spmd

    a = {k.split("_", 2)[2]: np.asarray(v) for k, v in inputs.items() if k.startswith("L0_attn_")}
    f = {k.split("_", 2)[2]: np.asarray(v) for k, v in inputs.items() if k.startswith("L0_ffn_")}
    by_block = lambda v: np.ascontiguousarray(v.reshape(-1, P).T)
    arrays = {
        "x": a["x"].reshape(L, D), "w_in": a["in_proj_w"].T, "w_out": a["out_proj_w"].T, "w_x": a["x_proj_w"].T,
        "w_router": f["w_router"],
        "a_log": a["A_log"].reshape(NG, GC, NM, SP).transpose(3, 1, 0, 2).reshape(P, NG, NM),
        "conv_w": a["conv_w"], "dt_w": by_block(a["dt_proj_w"]),
        "dt_b": by_block(a["dt_proj_b"]), "d_skip": by_block(a["D"]), "n_w": by_block(a["norm_w"]),
        "n_b": by_block(a["norm_b"]), "w1": f["w1"].reshape(E * D, H), "w2": f["w2"].reshape(E * H, D),
        "b1": f["b1"].reshape(E, HB, P).transpose(2, 1, 0), "b2": f["b2"], "consts": constants(),
    }
    nc = bacc.Bacc("TRN2", target_bir_lowering=False, num_devices=1)
    arrays = {f"in_{k}": np.ascontiguousarray(v) for k, v in arrays.items()}
    io = {k[3:]: nc.dram_tensor(k, v.shape, mybir.dt.from_np(v.dtype), kind="ExternalInput").ap()
          for k, v in arrays.items()}
    out = nc.dram_tensor("out", (L, D), F32, kind="ExternalOutput").ap()
    program(nc, io, out)
    r = run_bass_kernel_spmd(nc, [arrays], core_ids=[0])
    return r.results[0]["out"].reshape(1, L, D)
```
